# Optimizing a Trainium2 kernel written in Bass

```python
import numpy as np
import jax
import jax.numpy as jnp

def _softmax(x, axis=-1):
    return jax.nn.softmax(x, axis=axis)

def _gelu(x):
    return jax.nn.gelu(x, approximate=True)

def _silu(x):
    return jax.nn.silu(x)

def _sigmoid(x):
    return jax.nn.sigmoid(x)

def _layernorm(x, axis=-1, eps=1e-05):
    m = jnp.mean(x, axis=axis, keepdims=True)
    v = jnp.var(x, axis=axis, keepdims=True)
    return (x - m) / jnp.sqrt(v + eps)

def _scatter_add(tgt, idx, src, axis=0):
    return tgt.at[idx].add(src)

def _segment_sum(src, seg, n):
    return jax.ops.segment_sum(src, seg, n)
kernel_name = 'mk_flamingo_gated_d2_seqx_r8_f0686b'

def setup_inputs(seed: int=0):
    np.random.seed(seed)
    _w = jnp.asarray

    def _rec_inputs():
        import jax
        import jax.numpy as jnp
        _rk = jax.random.key(seed)
        x = 0.0002417 + 0.9998 * jax.random.normal(jax.random.fold_in(_rk, 1), (2, 512, 128), jnp.float32)
        _lenS = 512 - jax.random.randint(jax.random.fold_in(_rk, 7), (2,), 0, max(1, 512 // 4) + 1, jnp.int32)
        _lenS2 = 32 - jax.random.randint(jax.random.fold_in(_rk, 8), (2,), 0, max(1, 32 // 4) + 1, jnp.int32)
        _ctx_1024P = jax.random.normal(jax.random.fold_in(_rk, 11), (2, 16, 128), jnp.float32)
        _ctx_1024c = jax.random.dirichlet(jax.random.fold_in(_rk, 511), 0.3 * jnp.ones((16,), jnp.float32), (2, 32))
        _ctx_1024t = jnp.einsum('bsk,bkd->bsd', _ctx_1024c, _ctx_1024P)
        _ctx_1024t = _ctx_1024t * jax.lax.rsqrt(jnp.mean(jnp.square(_ctx_1024t)) + 1e-12) * 0.953939
        ctx_1024 = 7.22013e-05 + 1.00017 * (_ctx_1024t + 0.3 * jax.random.normal(jax.random.fold_in(_rk, 611), (2, 32, 128), jnp.float32))
        _g = jax.random.normal(jax.random.fold_in(_rk, 9001), (2, 2), jnp.float32)
        _g = jnp.sign(_g) * jnp.maximum(jnp.abs(_g), 1.0) + (_g == 0) * 1.0
        g_xattn = _g[0]
        g_ffn = _g[1]
        return (x, ctx_1024, g_xattn, g_ffn)
    x, ctx_1024, g_xattn, g_ffn = _rec_inputs()

    def _L0_xattn_setup():
        import jax, jax.numpy as jnp
        import numpy as np
        EMBED = 128
        HEADS = 16
        HEAD_DIM = EMBED // HEADS
        EXP_DIM = 2 * HEAD_DIM

        def _feature_map(x, fm_w, fm_b):
            z = jnp.einsum('nshd,ed->nshe', x, fm_w) + fm_b
            return jnp.concatenate([jnp.exp(z), jnp.exp(-z)], axis=-1)
        key = jax.random.key(seed)
        ks = jax.random.split(key, 7)
        N, S = (4, 256)
        values = jax.random.normal(ks[0], (N, S, EMBED), dtype=jnp.float32)
        keys_ = jax.random.normal(ks[1], (N, S, EMBED), dtype=jnp.float32)
        query = jax.random.normal(ks[2], (N, S, EMBED), dtype=jnp.float32)
        fm_w = jnp.eye(HEAD_DIM, dtype=jnp.float32) + 0.02 * jax.random.normal(ks[3], (HEAD_DIM, HEAD_DIM), dtype=jnp.float32)
        fm_b = 0.02 * jax.random.normal(ks[4], (HEAD_DIM,), dtype=jnp.float32)
        fc_w = jax.random.normal(ks[5], (EMBED, HEADS * EXP_DIM), dtype=jnp.float32) * (1.0 / np.sqrt(HEADS * EXP_DIM))
        fc_b = jnp.zeros((EMBED,), dtype=jnp.float32)
        return {'values': values, 'keys': keys_, 'query': query, 'fm_w': fm_w, 'fm_b': fm_b, 'fc_w': fc_w, 'fc_b': fc_b}
    _L0_xattn_all = _L0_xattn_setup()
    _L0_xattn_in = {k: v for k, v in _L0_xattn_all.items() if k in ('fm_w', 'fm_b', 'fc_w', 'fc_b')}
    del _L0_xattn_all

    def _L0_ffn_setup():
        import jax, jax.numpy as jnp
        import numpy as np
        S, B, H = (256, 1, 128)
        E, K, F = (8, 2, 176)
        key = jax.random.key(seed)
        k1, k2, k3, k4 = jax.random.split(key, 4)
        return {'hidden_states': jax.random.normal(k1, (S, B, H), jnp.float32), 'router_weight': jax.random.normal(k2, (H, E), jnp.float32) * 0.02, 'w1': jax.random.normal(k3, (E, H, 2 * F), jnp.float32) * 0.02, 'w2': jax.random.normal(k4, (E, F, H), jnp.float32) * 0.02}
    _L0_ffn_all = _L0_ffn_setup()
    _L0_ffn_in = {k: v for k, v in _L0_ffn_all.items() if k in ('router_weight', 'w1', 'w2')}
    del _L0_ffn_all

    def _L1_xattn_setup():
        import jax, jax.numpy as jnp
        import numpy as np
        D_MODEL = 128
        B, S = (4, 256)
        key = jax.random.key(seed)
        ks = jax.random.split(key, 10)
        s = 1.0 / np.sqrt(D_MODEL)
        return {'k': jax.random.normal(ks[0], (B, S, D_MODEL), jnp.float32), 'v': jax.random.normal(ks[1], (B, S, D_MODEL), jnp.float32), 'q': jax.random.normal(ks[2], (B, S, D_MODEL), jnp.float32), 'Wk': jax.random.normal(ks[3], (D_MODEL, D_MODEL), jnp.float32) * s, 'Wv': jax.random.normal(ks[4], (D_MODEL, D_MODEL), jnp.float32) * s, 'bv': jnp.zeros((D_MODEL,), jnp.float32), 'Wq': jax.random.normal(ks[5], (D_MODEL, D_MODEL), jnp.float32) * s, 'bq': jnp.zeros((D_MODEL,), jnp.float32), 'Wo': jax.random.normal(ks[6], (D_MODEL, D_MODEL), jnp.float32) * s, 'bo': jnp.zeros((D_MODEL,), jnp.float32)}
    _L1_xattn_all = _L1_xattn_setup()
    _L1_xattn_in = {k: v for k, v in _L1_xattn_all.items() if k in ('Wk', 'Wv', 'bv', 'Wq', 'bq', 'Wo', 'bo')}
    del _L1_xattn_all

    def _L1_ffn_setup():
        import jax, jax.numpy as jnp
        import numpy as np
        B, S, D = (4, 256, 128)
        E, H, TOP_K = (8, 256, 2)
        key = jax.random.key(seed)
        k_x, k_g, k_w1, k_w2, k_w3 = jax.random.split(key, 5)
        s_d = 1.0 / np.sqrt(D)
        s_h = 1.0 / np.sqrt(H)
        return {'x': jax.random.normal(k_x, (B, S, D), dtype=jnp.float32), 'w_gate': jax.random.normal(k_g, (D, E), dtype=jnp.float32) * s_d, 'w1': jax.random.normal(k_w1, (E, D, H), dtype=jnp.float32) * s_d, 'w3': jax.random.normal(k_w3, (E, D, H), dtype=jnp.float32) * s_d, 'w2': jax.random.normal(k_w2, (E, H, D), dtype=jnp.float32) * s_h}
    _L1_ffn_all = _L1_ffn_setup()
    _L1_ffn_in = {k: v for k, v in _L1_ffn_all.items() if k in ('w_gate', 'w1', 'w3', 'w2')}
    del _L1_ffn_all
    return {'x': x, 'ctx_1024': ctx_1024, 'g_xattn': g_xattn, 'g_ffn': g_ffn, 'L0_xattn_fm_w': _L0_xattn_in['fm_w'], 'L0_xattn_fm_b': _L0_xattn_in['fm_b'], 'L0_xattn_fc_w': _L0_xattn_in['fc_w'], 'L0_xattn_fc_b': _L0_xattn_in['fc_b'], 'L0_ffn_router_weight': _L0_ffn_in['router_weight'], 'L0_ffn_w1': _L0_ffn_in['w1'], 'L0_ffn_w2': _L0_ffn_in['w2'], 'L1_xattn_Wk': _L1_xattn_in['Wk'], 'L1_xattn_Wv': _L1_xattn_in['Wv'], 'L1_xattn_bv': _L1_xattn_in['bv'], 'L1_xattn_Wq': _L1_xattn_in['Wq'], 'L1_xattn_bq': _L1_xattn_in['bq'], 'L1_xattn_Wo': _L1_xattn_in['Wo'], 'L1_xattn_bo': _L1_xattn_in['bo'], 'L1_ffn_w_gate': _L1_ffn_in['w_gate'], 'L1_ffn_w1': _L1_ffn_in['w1'], 'L1_ffn_w3': _L1_ffn_in['w3'], 'L1_ffn_w2': _L1_ffn_in['w2']}

def reference(x, ctx_1024, g_xattn, g_ffn, L0_xattn_fm_w, L0_xattn_fm_b, L0_xattn_fc_w, L0_xattn_fc_b, L0_ffn_router_weight, L0_ffn_w1, L0_ffn_w2, L1_xattn_Wk, L1_xattn_Wv, L1_xattn_bv, L1_xattn_Wq, L1_xattn_bq, L1_xattn_Wo, L1_xattn_bo, L1_ffn_w_gate, L1_ffn_w1, L1_ffn_w3, L1_ffn_w2):
    import jax
    import jax.numpy as jnp

    def _L0_xattn_ref(values, keys, query, fm_w, fm_b, fc_w, fc_b):
        import jax, jax.numpy as jnp
        import numpy as np
        EMBED = 128
        HEADS = 16
        HEAD_DIM = EMBED // HEADS
        EXP_DIM = 2 * HEAD_DIM

        def _feature_map(x, fm_w, fm_b):
            z = jnp.einsum('nshd,ed->nshe', x, fm_w) + fm_b
            return jnp.concatenate([jnp.exp(z), jnp.exp(-z)], axis=-1)
        N, S, _ = query.shape
        v = values.reshape(N, -1, HEADS, HEAD_DIM)
        k = keys.reshape(N, -1, HEADS, HEAD_DIM)
        q = query.reshape(N, -1, HEADS, HEAD_DIM)
        v, k, q = (_feature_map(x, fm_w, fm_b) for x in (v, k, q))
        scores = jnp.einsum('nqhd,nkhd->nhqk', q, k) / jnp.sqrt(jnp.float32(EMBED))
        attn = jax.nn.softmax(scores, axis=-1)
        out = jnp.einsum('nhql,nlhd->nqhd', attn, v)
        out = out.reshape(N, S, HEADS * EXP_DIM)
        return out @ fc_w.T + fc_b

    def _L0_ffn_ref(hidden_states, router_weight, w1, w2):
        import jax, jax.numpy as jnp
        import numpy as np
        S, B, H = (256, 1, 128)
        E, K, F = (8, 2, 176)
        s, b, h = hidden_states.shape
        x = hidden_states.reshape(-1, h)
        logits = x @ router_weight
        probs = jax.nn.softmax(logits, axis=-1)
        _, topk_idx = jax.lax.top_k(probs, K)
        routing_map = jax.nn.one_hot(topk_idx, E, dtype=probs.dtype).sum(axis=1)
        local_probs = probs * routing_map
        y = jnp.einsum('th,ehf->tef', x, w1)
        y1, y2 = jnp.split(y, 2, axis=-1)
        g = jax.nn.silu(y1) * y2
        o = jnp.einsum('tef,efh->teh', g, w2)
        out = jnp.einsum('teh,te->th', o, local_probs)
        return out.reshape(s, b, h)

    def _L1_xattn_ref(k, v, q, Wk, Wv, bv, Wq, bq, Wo, bo):
        import jax, jax.numpy as jnp
        import numpy as np
        D_MODEL = 128
        B, S = (4, 256)
        kp = jnp.einsum('bsd,ed->bse', k, Wk)
        vp = jnp.einsum('bsd,ed->bse', v, Wv) + bv
        qp = jnp.einsum('bsd,ed->bse', q, Wq) + bq
        scale = 1.0 / jnp.sqrt(jnp.float32(kp.shape[-1]))
        scores = jnp.einsum('bqd,bkd->bqk', qp, kp) * scale
        probs = jax.nn.softmax(scores, axis=-1)
        ctx = jnp.einsum('bqk,bkd->bqd', probs, vp)
        return jnp.einsum('bqd,ed->bqe', ctx, Wo) + bo

    def _L1_ffn_ref(x, w_gate, w1, w3, w2):
        import jax, jax.numpy as jnp
        import numpy as np
        B, S, D = (4, 256, 128)
        E, H, TOP_K = (8, 256, 2)
        bsz, seq_len, embed_dim = x.shape
        xt = x.reshape(-1, embed_dim)
        T = xt.shape[0]
        logits = xt @ w_gate
        top_logits, sel = jax.lax.top_k(logits, TOP_K)
        probs = jax.nn.softmax(top_logits, axis=-1).astype(x.dtype)
        h = jax.nn.silu(jnp.einsum('td,edh->eth', xt, w1)) * jnp.einsum('td,edh->eth', xt, w3)
        y = jnp.einsum('eth,ehd->etd', h, w2)
        t_idx = jnp.arange(T)
        yk = y[sel.T, t_idx[None, :], :]
        out = jnp.einsum('ktd,tk->td', yk, probs)
        return out.reshape(bsz, seq_len, embed_dim)
    x = x + jnp.tanh(g_xattn[0]) * _L0_xattn_ref(ctx_1024, ctx_1024, _layernorm(x, axis=-1), L0_xattn_fm_w, L0_xattn_fm_b, L0_xattn_fc_w, L0_xattn_fc_b)
    x = x + jnp.tanh(g_ffn[0]) * _L0_ffn_ref(_layernorm(x, axis=-1), L0_ffn_router_weight, L0_ffn_w1, L0_ffn_w2)
    x = x + jnp.tanh(g_xattn[1]) * _L1_xattn_ref(ctx_1024, ctx_1024, _layernorm(x, axis=-1), L1_xattn_Wk, L1_xattn_Wv, L1_xattn_bv, L1_xattn_Wq, L1_xattn_bq, L1_xattn_Wo, L1_xattn_bo)
    x = x + jnp.tanh(g_ffn[1]) * _L1_ffn_ref(_layernorm(x, axis=-1), L1_ffn_w_gate, L1_ffn_w1, L1_ffn_w3, L1_ffn_w2)
    return x

_drawn_inputs = setup_inputs


def setup_inputs(seed=0):
    import zlib

    import numpy as np

    out = dict(_drawn_inputs(seed))
    spreads = {'g_ffn': (-1.0, 0.6),
     'L0_xattn_fc_b': (0.0, 0.8),
     'L1_xattn_bv': (0.0, 0.8),
     'L1_xattn_bq': (0.0, 0.8),
     'L1_xattn_bo': (0.0, 0.8)}
    factors = {'L0_ffn_router_weight': 8.0,
     'L0_ffn_w1': 8.0,
     'L0_ffn_w2': 8.0,
     'L1_xattn_Wk': 3.784,
     'L1_xattn_Wq': 2.743}
    for name, (base, spread) in spreads.items():
        noise = np.random.default_rng([zlib.crc32(name.encode()), seed]).standard_normal(out[name].shape)
        drawn = base * np.exp(spread * noise) if base else spread * noise
        out[name] = jnp.asarray(drawn.astype(out[name].dtype))
    for name, factor in factors.items():
        out[name] = (out[name] * factor).astype(out[name].dtype)
    return out
```

```python
import concourse.bass as bass
from concourse import mybir
from contextlib import ExitStack

P = 128
D = 128
TOK = 512
NT = TOK // P
NG = 2
KEYS = 32
HEADS, HD = 16, 8
HG = 8
E = 8
FF = (176, 256)
NCH = tuple(E * f // P for f in FF)
EPS = 1e-5
SCALE = 1.0 / float(D) ** 0.5
NY = 3

NA = 3
HID_EXPERTS = (8, 3)

MM1_STEPS = 2 * E


def chunk_steps(layer):
    steps = []
    for c in range(NCH[layer]):
        last_expert = (c * P + P - 1) // FF[layer]
        steps.append(max(2 * last_expert + 2, steps[-1] + 1 if steps else 0))
    return steps


TSTEP = (chunk_steps(0), chunk_steps(1))
TAIL = tuple(s[-1] + 2 for s in TSTEP)
A_STEPS = (15, 8)
WPIECES = 18


def chunks_before(n):
    return sum(NCH[m // 2] for m in range(n))


def slots():
    order = []
    weights = list(range(WPIECES))
    for k in range(A_STEPS[0]):
        order.append(("A", 0, k))
        if 3 <= k < 9:
            order.append(("W", 0, weights.pop(0)))
    for n in range(4):
        steps = TAIL[n // 2] + 2
        for k in range(steps):
            order.append(("F", n, k))
            if weights and k < MM1_STEPS:
                order.append(("W", 0, weights.pop(0)))
            if n < 3 and k < A_STEPS[(n + 1) // 2]:
                order.append(("A", n + 1, k))
    return order


SLOTS = slots()


def build(nc, x_d, ctx_d, gx_d, gf_d, fmw_d, fmb_d, fcw_d, fcb_d, rw0_d, w1_d, w2_d,
          wk_d, wv_d, bv_d, wq_d, bq_d, wo_d, bo_d, rw1_d, u1_d, u3_d, u2_d, out_d):
    f32, f32r = mybir.dt.float32, mybir.dt.float32r
    ALU, ACT, AX = mybir.AluOpType, mybir.ActivationFunctionType, mybir.AxisListType
    stack = ExitStack()
    with stack:
        def sb(name, shape, dt=f32):
            return stack.enter_context(nc.sbuf_tensor(name, shape, dt))

        def sem(name):
            return stack.enter_context(nc.semaphore(name))

        x_sb = sb("x_sb", [P, NG * NT, D])
        stats = sb("stats", [P, NT, 6])
        mv = sb("mv", [P, NT, 2])
        rstd = sb("rstd", [P, NT])
        varp = sb("varp", [P, NT])
        half = sb("half", [P, NT])
        xn = sb("xn", [P, NT, D])
        xa = [sb(f"xa{i}", [P, TOK], f32r) for i in "hl"]
        xf = [[sb(f"xf{g}{i}", [P, TOK], f32r) for i in "hl"] for g in range(NG)]

        ident = sb("ident", [P, P])
        ones = sb("ones", [1, P])
        sgn_mask = sb("sgn_mask", [P, 2, 2, HG * HD])
        key_mask = sb("key_mask", [P, HG, KEYS])
        rep = sb("rep", [HD, P])
        rep_sgn = sb("rep_sgn", [HD, P])
        fm_t = sb("fm_t", [HD, HD])
        fm_b = sb("fm_b", [HD, 1])
        wz = sb("wz", [P, 2, P])
        wzs = [sb(f"wz{i}", [P, 2, P], f32r) for i in "hl"]
        bz = sb("bz", [P, 1])
        ctx_sb = sb("ctx_sb", [NG * KEYS, D])
        ctx_t = sb("ctx_t", [D, NG * KEYS])
        fk = sb("fk", [P, 2, NG * KEYS])
        fks = [sb(f"fk{i}", [P, 2, NG * KEYS], f32r) for i in "hl"]
        kbd = [sb(f"kbd{i}", [P, NG, 2, HG, KEYS], f32r) for i in "hl"]
        fcs = [sb(f"fc{i}", [P, 2, D], f32r) for i in "hl"]
        fcb = sb("fcb", [1, D])
        v0 = sb("v0", [P, NG, 4, D])
        gates = sb("gates", [P, 4])
        tg = sb("tg", [P, 4])

        wq, wk, wv, wo = (sb(n, [D, D]) for n in ("wq", "wk", "wv", "wo"))
        bq, bv = sb("bq", [D, 1]), sb("bv", [D, 1])
        wo_t = sb("wo_t", [D, D])
        kq = sb("kq", [D, D])
        vo = sb("vo", [D, D])
        bqk = sb("bqk", [D, 1])
        bvo = sb("bvo", [1, D])
        m1s = [sb(f"m1{i}", [D, NG * KEYS], f32r) for i in "hl"]
        c1 = sb("c1", [1, NG * KEYS])
        v1 = sb("v1", [KEYS + 1, NG, D])

        qfs = [sb(f"qf{i}", [P, 2, TOK], f32r) for i in "hl"]
        nmax = sb("nmax", [P, NT, HEADS])
        prob = sb("prob", [P, NT, HEADS * KEYS])
        qf = prob[:, 0:2, :]
        fc_sb = prob[:, 2, 0:256].rearrange("n (g h s e) -> n g h s e", g=2, h=HG, s=2)
        fc_p = prob[:, 2, 256:512].rearrange("n (g s h e) -> n g s h e", g=2, s=2, h=HG)
        psum_ = sb("psum_", [P, NT, HEADS])
        prec = sb("prec", [P, NT, HEADS])
        prob_t = sb("prob_t", [P, 2, 4, P])
        prob1 = sb("prob1", [P, NT, KEYS + 1])
        nmax1, sum1, rec1 = sb("nmax1", [P, NT]), sb("sum1", [P, NT]), sb("rec1", [P, NT])
        prob1_t = sb("prob1_t", [KEYS + 1, NT, P])

        rw = sb("rw", [D, 2, E])
        rws = [sb(f"rw{i}", [D, 2, E], f32r) for i in "hl"]
        logit = sb("logit", [P, NT, E])
        before = sb("before", [P, E, E])
        cmp_gt = sb("cmp_gt", [P, NT, E, E])
        cmp_eq = sb("cmp_eq", [P, NT, E, E])
        rank = sb("rank", [P, NT, E])
        lmax = sb("lmax", [P, NT])
        ldiff = sb("ldiff", [P, NT, E])
        lexp = sb("lexp", [P, NT, E])
        lsel = sb("lsel", [P, NT, E])
        lsum, lrec = sb("lsum", [P, NT]), sb("lrec", [P, NT])
        route = [sb(f"route{g}", [P, NT, E]) for g in range(NG)]

        stage = sb("stage", [P, 2 * E * FF[0] + NCH[0] * P])
        wa_f = [stage[:, 0:2 * E * ff].rearrange("p (e s f) -> p e s f", e=E, s=2) for ff in FF]
        wb_f = [stage[:, 2 * E * FF[0]:].rearrange("p (c n) -> p c n", n=D),
                stage[:, 0:NCH[1] * D].rearrange("p (c n) -> p c n", n=D)]
        wa_l = [sb(f"wal{l}", [D, E, 2, FF[l]], f32r) for l in range(2)]
        wa_h = [sb(f"wah{l}", [D, E, 2, FF[l]], f32r) for l in range(2)]
        wb_h = [sb(f"wbh{l}", [P, NCH[l], D], f32r) for l in range(2)]
        wb_l = [sb(f"wbl{l}", [P, NCH[l], D], f32r) for l in range(2)]
        act_sb = sb("act_sb", [P, NA, FF[1]])
        hid = sb("hid", [P, NT, NCH[0] * P])
        hid_t = [sb(f"hid_t{i}", [P, 2, TOK], f32r) for i in "hl"]
        o_t = sb("o_t", [D, TOK])

        bank = [stack.enter_context(nc.psum_tensor(f"bank{i}", [P, 512], f32)) for i in range(8)]
        yb, tb, ob = bank[0:NY], bank[3], bank[4]
        ba, bs, bp = bank[5], bank[6], bank[7]

        names = """ld_x0 ld_x1 ld_ctx ld_fm ld_fc ld_g ld_r ld_at ld_bo ld_w0 ld_w1 ld_w2 ld_w3 ld_w4 ld_w5 ld_w6 ld_w7 ld_w8 ld_w9 out_done
            const_ready pool_own rstd_ready var_ready
            wzp_done wz_done wzh_done wzl_done bz_done ctxT_done ctxT_sb zk_done fk_done fkh_done fkl_done
            kbdh_done kbdl_done fcp_done fcT_done fch_done fcl_done v0_done v0_sb tg_done
            l1_pe l1_sb one_col rw_h rw_l
            stats_ready mv_ready xn_ready xT_ready xh_ready xl_ready
            z_ready qf_ready qh_ready ql_ready score_ready nmax_ready shifted exp_ready sum_ready rec_ready
            prob_ready probT_ready probT_sb att_ready x_att
            s1_ready s1_nmax s1_shift s1_exp s1_sum s1_rec s1_prob s1_T s1_T_sb
            logit_ready logit_sb router_dve lexp_ready route_ready
            wsplit_h wsplit_l
            y_ready act_ready hid_ready hidT_ready hidh_ready hidl_ready mm2_done o_sb oT_ready x_ffn"""
        S = {n: sem(n) for n in names.split()}

        block = stack.enter_context(nc.Block())

        def flat(t):
            return t.rearrange("p e s f -> p e (s f)")

        pieces = []
        for q in range(4):
            pieces.append([v[:, 2 * q:2 * q + 2, :] for v in (flat(wa_f[0]), flat(wa_h[0][:, :, :, :]), flat(wa_l[0][:, :, :, :]))])
        for a, b in ((0, 6), (6, NCH[0])):
            pieces.append([v[:, a:b, :] for v in (wb_f[0], wb_h[0], wb_l[0])])
        for q in range(8):
            pieces.append([v[:, q:q + 1, :] for v in (flat(wa_f[1]), flat(wa_h[1][:, :, :, :]), flat(wa_l[1][:, :, :, :]))])
        for q in range(4):
            pieces.append([v[:, 4 * q:4 * q + 4, :] for v in (wb_f[1], wb_h[1], wb_l[1])])
        assert len(pieces) == WPIECES
        load_of = [0, 1, 2, 3, 4, 4] + [5, 5, 6, 6, 7, 7, 8, 8] + [9] * 4
        landed = [32 if 5 <= i <= 8 else 16 for i in load_of]
        def wa_pieces(layer, e):
            return e // 2 + 1 if layer == 0 else 6 + e + 1

        def wb_pieces(layer, c):
            return (5 if c < 6 else 6) if layer == 0 else 14 + c // 4 + 1

        @block.sync
        def _(sp):
            def load(dst, src, s):
                sp.dma_start(dst, src).then_inc(S[s], 16)
            load(ctx_sb[:, :], ctx_d.rearrange("b k d -> (b k) d"), "ld_ctx")
            load(x_sb[:, 0:NT, :], x_d[0].rearrange("(t p) d -> p t d", p=P), "ld_x0")
            load(fc_sb[:, :, :, :, :], fcw_d.rearrange("n (g h s e) -> n g h s e", g=2, h=HG, s=2), "ld_fc")
            load(fcb[:, :], fcb_d.rearrange("(a n) -> a n", a=1), "ld_fc")
            for q in range(4):
                load(wa_f[0][:, 2 * q:2 * q + 2, :, :].rearrange("p e s f -> p e (s f)"),
                     w1_d[2 * q:2 * q + 2].rearrange("e p f -> p e f"), f"ld_w{q}")
            load(wb_f[0][:, :, :], w2_d.rearrange("e f n -> (e f) n").rearrange("(c p) n -> p c n", p=P), "ld_w4")
            load(x_sb[:, NT:2 * NT, :], x_d[1].rearrange("(t p) d -> p t d", p=P), "ld_x1")
            for q in range(4):
                if q == 0:
                    sp.wait_ge(S["wsplit_l"], 4)
                if q == 2:
                    sp.wait_ge(S["wsplit_l"], 6)
                for s, w in enumerate((u1_d, u3_d)):
                    load(wa_f[1][:, 2 * q:2 * q + 2, s, :], w[2 * q:2 * q + 2].rearrange("e p f -> p e f"), f"ld_w{5 + q}")
            sp.wait_ge(S["wsplit_l"], 10)
            load(wb_f[1][:, :, :], u2_d.rearrange("e f n -> (e f) n").rearrange("(c p) n -> p c n", p=P), "ld_w9")
            for g in range(NG):
                sp.wait_ge(S["x_ffn"], NG + g + 1)
                sp.dma_start(out_d[g].rearrange("(t p) d -> p t d", p=P),
                             x_sb[:, g * NT:(g + 1) * NT, :]).then_inc(S["out_done"], 16)
            sp.wait_ge(S["out_done"], 16 * NG)

        @block.gpsimd
        def _(pool):
            def load(dst, src, s):
                pool.dma_start(dst, src).then_inc(S[s], 16)
            pool.dma_start(fm_t[:, :], fmw_d.rearrange("e d -> d e"), allow_slow_non_contiguous=True).then_inc(S["ld_fm"], 16)
            load(fm_b[:, :], fmb_d.rearrange("(d a) -> d a", a=1), "ld_fm")
            for i, g in enumerate((gx_d, gf_d)):
                load(gates[:, 2 * i:2 * i + 2], g.rearrange("(a n) -> a n", a=1).to_broadcast([P, 2]), "ld_g")
            load(rw[:, 0, :], rw0_d, "ld_r")
            load(rw[:, 1, :], rw1_d, "ld_r")

            own = [0]

            def step(ins):
                own[0] += 1
                ins.then_inc(S["pool_own"], 1)
                pool.wait_ge(S["pool_own"], own[0])

            def select(ap, pattern, base, cm, op, fill):
                return pool.affine_select(out=ap, in_=ap, compare_op=op, fill=fill, base=base,
                                          pattern=pattern, channel_multiplier=cm)

            step(pool.memset(ident[:, :], 0.0))
            select(ident[:, :], [[-1, P]], 0, 1, ALU.not_equal, 1.0).then_inc(S["const_ready"], 1)
            pool.memset(rep[:, :], 0.0)
            step(pool.memset(rep_sgn[:, :], 0.0))
            select(rep[:, :].rearrange("p (h d) -> p h d", d=HD), [[0, HEADS], [-1, HD]], 0, 1,
                   ALU.not_equal, 1.0).then_inc(S["const_ready"], 1)
            for s, sign in enumerate((1.0, -1.0)):
                select(rep_sgn[:, s * 64:s * 64 + 64].rearrange("p (h d) -> p h d", d=HD), [[0, HG], [-1, HD]], 0, 1,
                       ALU.not_equal, sign).then_inc(S["const_ready"], 1)
            pool.memset(sgn_mask[:, :, 0, :], 1.0)
            step(pool.memset(sgn_mask[:, :, 1, :], -1.0))
            for g in range(2):
                v = sgn_mask[:, g, :, :].rearrange("p s (h e) -> p s h e", e=HD)
                step(select(v, [[0, 2], [-HD, HG], [0, HD]], -64 * g, 1, ALU.is_ge, 0.0))
                select(v, [[0, 2], [HD, HG], [0, HD]], 64 * g + HD - 1, -1, ALU.is_ge, 0.0)\
                    .then_inc(S["const_ready"], 1)
            pool.memset(half[:, :], -0.5)
            pool.memset(ones[:, :], 1.0).then_inc(S["const_ready"], 1)
            step(pool.memset(key_mask[:, :, :], 1.0))
            for r in range(2):
                v = key_mask[64 * r:64 * r + 64, :, :]
                step(select(v, [[-HD, HG], [0, KEYS]], 0, 1, ALU.is_ge, 0.0))
                select(v, [[HD, HG], [0, KEYS]], HD - 1, -1, ALU.is_ge, 0.0).then_inc(S["const_ready"], 1)
                pool.wait_ge(S["const_ready"], 8 + r)
            step(pool.memset(before[:, :, :], 1.0))
            select(before[:, :, :], [[1, E], [-1, E]], 0, 0, ALU.is_gt, 0.0).then_inc(S["const_ready"], 1)
            pool.memset(prob1[:, :, KEYS:KEYS + 1], 1.0).then_inc(S["one_col"], 1)
            pool.wait_ge(S["ld_fc"], 32)
            for g in range(2):
                pool.tensor_copy(fc_p[:, g], fc_sb[:, g].rearrange("n h s e -> n s h e")).then_inc(S["fcp_done"], 1)

            def rstd_of(m):
                pool.wait_ge(S["mv_ready"], NT * (m + 1))
                step(pool.tensor_scalar(varp[:, :], mv[:, :, 1], EPS, None, ALU.add))
                pool.tensor_tensor(rstd[:, :], varp[:, :], half[:, :], ALU.pow).then_inc(S["rstd_ready"], 1)

            def attention(n, k):
                if k == 0:
                    rstd_of(2 * n)
                if n < 2:
                    if k == 7:
                        for t in range(NT):
                            pool.wait_ge(S["rec_ready"], NT * n + t + 1)
                            v = prob[:, t, :].rearrange("p (h k) -> p h k", k=KEYS)
                            pool.tensor_tensor(v, v, prec[:, t, :].unsqueeze(2).to_broadcast([P, HEADS, KEYS]),
                                               ALU.mult).then_inc(S["prob_ready"], 1)
                    if k == 12:
                        rstd_of(2 * n + 1)
                elif k == 5:
                    rstd_of(2 * n + 1)

            def split(i):
                full, h, l = pieces[i]
                pool.wait_ge(S["wsplit_h"], i + 1)
                pool.tensor_tensor(l, full, h.bitcast(f32), ALU.subtract).then_inc(S["wsplit_l"], 1)

            first = True
            for kind, n, k in SLOTS:
                if kind == "A":
                    attention(n, k)
                elif kind == "W":
                    split(k)
                if first:
                    first = False
                    pool.wait_ge(S["fkl_done"], 1)
                    for b in range(NG):
                        for g in range(2):
                            pool.tensor_tensor(kbd[1][:, b, g], key_mask[:, :, :],
                                               fks[1][:, g, b * KEYS:(b + 1) * KEYS].bitcast(f32).unsqueeze(1)
                                               .to_broadcast([P, HG, KEYS]), ALU.mult).then_inc(S["kbdl_done"], 1)

        @block.scalar
        def _(act):
            def load(dst, src):
                act.dma_start(dst, src).then_inc(S["ld_at"], 16)
            for dst, src in ((wq, wq_d), (wk, wk_d), (wv, wv_d), (wo, wo_d)):
                load(dst[:, :], src)
            for dst, src in ((bq, bq_d), (bv, bv_d)):
                load(dst[:, :], src.rearrange("(d a) -> d a", a=1))
            for b in range(NG):
                act.dma_start(v1[KEYS:KEYS + 1, b, :], bo_d.rearrange("(a n) -> a n", a=1)).then_inc(S["ld_bo"], 16)

            def copy(dst, src):
                return nc.scalar.activation(dst, src, ACT.Copy)

            act.wait_ge(S["ctxT_done"], 1)
            copy(ctx_t[:, :], ba[:, 0:NG * KEYS]).then_inc(S["ctxT_sb"], 1)
            act.wait_ge(S["wz_done"], 1)
            copy(wzs[0][:, :, :], wz[:, :, :]).then_inc(S["wzh_done"], 1)
            act.wait_ge(S["bz_done"], 1)
            copy(bz[:, :], bs[:, 0:1]).then_inc(S["bz_done"], 1)
            act.wait_ge(S["zk_done"], 1)
            act.wait_ge(S["bz_done"], 2)
            nc.scalar.activation(fk[:, :, :].rearrange("p g k -> p (g k)"), bp[:, 0:2 * NG * KEYS], ACT.Exp,
                                 bias=bz[:, 0:1]).then_inc(S["fk_done"], 1)
            act.wait_ge(S["fk_done"], 1)
            copy(fks[0][:, :, :], fk[:, :, :]).then_inc(S["fkh_done"], 1)
            act.wait_ge(S["ld_g"], 32)
            nc.scalar.activation(tg[:, :], gates[:, :], ACT.Tanh).then_inc(S["tg_done"], 1)

            def prepare_values():
                act.wait_ge(S["fcT_done"], 1)
                copy(fcs[0][:, :, :].rearrange("p g n -> p (g n)"), ob[:, 0:2 * D]).then_inc(S["fch_done"], 1)
                for b in range(NG):
                    act.wait_ge(S["v0_done"], b + 1)
                    copy(v0[:, b, :, :].rearrange("p c n -> p (c n)"), yb[b][:, :]).then_inc(S["v0_sb"], 1)
                act.wait_ge(S["ld_r"], 32)
                copy(rws[0][:, :, :], rw[:, :, :]).then_inc(S["rw_h"], 1)

            def prepare_layer1(i):
                act.wait_ge(S["l1_pe"], i + 1)
                if i == 0:
                    copy(wo_t[:, :], yb[2][:, 0:D])
                    copy(kq[:, :], yb[2][:, D:2 * D])
                    copy(bqk[:, :], yb[2][:, 2 * D:2 * D + 1]).then_inc(S["l1_sb"], 1)
                elif i == 1:
                    copy(vo[:, :], tb[:, 0:D])
                    copy(bvo[:, :], tb[0:1, D:2 * D])
                    copy(m1s[0][:, :], tb[:, 256:256 + NG * KEYS])
                    copy(c1[:, :], tb[0:1, 384:384 + NG * KEYS]).then_inc(S["l1_sb"], 1)
                else:
                    copy(v1[0:KEYS, :, :].rearrange("k b n -> k (b n)"), ob[0:KEYS, 0:NG * D]).then_inc(S["l1_sb"], 1)

            def high_of_xT(m, dst):
                act.wait_ge(S["xT_ready"], m + 1)
                copy(dst[0][:, :], ba[:, :]).then_inc(S["xh_ready"], 1)

            def router_exp(n):
                act.wait_ge(S["router_dve"], 3 * n + 2)
                nc.scalar.activation(lexp[:, :, :], ldiff[:, :, :], ACT.Exp).then_inc(S["lexp_ready"], 1)

            def attention(n, k):
                g = n % 2
                if n < 2:
                    if k == 1:
                        high_of_xT(2 * n, xa)
                    if k == 2:
                        for h in range(2):
                            act.wait_ge(S["z_ready"], 2 * n + h + 1)
                            nc.scalar.activation(qf[:, h, :], (bs, bp)[h][:, :], ACT.Exp,
                                                 bias=bz[:, 0:1]).then_inc(S["qf_ready"], 1)
                        for h in range(2):
                            act.wait_ge(S["qf_ready"], 2 * n + h + 1)
                            copy(qfs[0][:, h, :], qf[:, h, :]).then_inc(S["qh_ready"], 1)
                    if k == 7:
                        for t in range(NT):
                            act.wait_ge(S["shifted"], NT * n + t + 1)
                            nc.scalar.activation(prob[:, t, :], prob[:, t, :], ACT.Exp,
                                                 scale=SCALE).then_inc(S["exp_ready"], 1)
                    if 8 <= k < 8 + NT:
                        t = k - 8
                        act.wait_ge(S["probT_ready"], NT * n + t + 1)
                        copy(prob_t[:, t % 2].rearrange("p c q -> p (c q)"), bp[:, :]).then_inc(S["probT_sb"], 1)
                    if k == 13:
                        high_of_xT(2 * n + 1, xf[g])
                    if k == 14:
                        router_exp(n)
                else:
                    if k == 1:
                        high_of_xT(2 * n, xa)
                    if k == 2:
                        act.wait_ge(S["s1_shift"], n - 1)
                        nc.scalar.activation(prob1[:, :, 0:KEYS], prob1[:, :, 0:KEYS], ACT.Exp,
                                             scale=SCALE).then_inc(S["s1_exp"], 1)
                    if k == 3:
                        act.wait_ge(S["s1_T"], n - 1)
                        copy(prob1_t[:, :, :].rearrange("k t q -> k (t q)"), bp[0:KEYS + 1, :]).then_inc(S["s1_T_sb"], 1)
                    if k == 6:
                        high_of_xT(2 * n + 1, xf[g])
                    if k == 7:
                        router_exp(n)

            def experts(n, k):
                layer, ff = n // 2, FF[n // 2]
                if k < MM1_STEPS:
                    for i in range(2):
                        y = 2 * (MM1_STEPS * n + k) + i
                        act.wait_ge(S["y_ready"], y + 1)
                        if y >= NA:
                            act.wait_ge(S["hid_ready"], y - NA + 1)
                        nc.scalar.activation(act_sb[:, y % NA, 0:ff], yb[y % NY][:, 0:ff], ACT.Silu)\
                            .then_inc(S["act_ready"], 1)
                if k in TSTEP[layer]:
                    c = chunks_before(n) + TSTEP[layer].index(k)
                    act.wait_ge(S["hidT_ready"], c + 1)
                    if c >= 2:
                        act.wait_ge(S["mm2_done"], c - 1)
                    copy(hid_t[0][:, c % 2, :], tb[:, :]).then_inc(S["hidh_ready"], 1)
                if k == TAIL[layer]:
                    act.wait_ge(S["mm2_done"], chunks_before(n + 1))
                    copy(o_t[:, :], ob[:, :]).then_inc(S["o_sb"], 1)

            def split(i):
                full, h, l = pieces[i]
                act.wait_ge(S[f"ld_w{load_of[i]}"], landed[i])
                copy(h, full).then_inc(S["wsplit_h"], 1)

            for kind, n, k in SLOTS:
                if kind == "A":
                    attention(n, k)
                    if (n, k) == (0, 2):
                        prepare_values()
                    if n == 0 and k in (9, 10, 11):
                        prepare_layer1(k - 9)
                elif kind == "W":
                    split(k)
                else:
                    experts(n, k)

        @block.vector
        def _(dve):
            V = nc.vector

            def low(dst, full, high, s):
                V.tensor_tensor(dst, full, high.bitcast(f32), ALU.subtract).then_inc(S[s], 1)

            dve.wait_ge(S["wzp_done"], 1)
            dve.wait_ge(S["const_ready"], 6)
            V.tensor_tensor(wz[:, :, :].rearrange("p g c -> p (g c)"), bs[:, 128:384],
                            sgn_mask[:, :, :, :].rearrange("p g s c -> p (g s c)"), ALU.mult).then_inc(S["wz_done"], 1)
            dve.wait_ge(S["wz_done"], 1)
            dve.wait_ge(S["wzh_done"], 1)
            low(wzs[1][:, :, :], wz[:, :, :], wzs[0][:, :, :], "wzl_done")

            def key_blocks():
                dve.wait_ge(S["fkh_done"], 1)
                low(fks[1][:, :, :], fk[:, :, :], fks[0][:, :, :], "fkl_done")
                dve.wait_ge(S["const_ready"], 10)
                for b in range(NG):
                    for g in range(2):
                        V.tensor_tensor(kbd[0][:, b, g], key_mask[:, :, :],
                                        fks[0][:, g, b * KEYS:(b + 1) * KEYS].bitcast(f32).unsqueeze(1)
                                        .to_broadcast([P, HG, KEYS]), ALU.mult).then_inc(S["kbdh_done"], 1)

            def prepare_values():
                dve.wait_ge(S["fch_done"], 1)
                low(fcs[1][:, :, :].rearrange("p g n -> p (g n)"), ob[:, 0:2 * D],
                    fcs[0][:, :, :].rearrange("p g n -> p (g n)"), "fcl_done")
                dve.wait_ge(S["rw_h"], 1)
                low(rws[1][:, :, :], rw[:, :, :], rws[0][:, :, :], "rw_l")

            def prepare_layer1():
                dve.wait_ge(S["l1_sb"], 2)
                low(m1s[1][:, :], tb[:, 256:256 + NG * KEYS], m1s[0][:, :], "l1_sb")

            def normalise(m, g):
                for t in range(NT):
                    V.bn_stats(stats[:, t, :], x_sb[:, g * NT + t, :]).then_inc(S["stats_ready"], 1)
                for t in range(NT):
                    dve.wait_ge(S["stats_ready"], NT * m + t + 1)
                    V.bn_aggr(mv[:, t, :], stats[:, t, :]).then_inc(S["mv_ready"], 1)
                dve.wait_ge(S["rstd_ready"], m + 1)
                if m:
                    dve.wait_ge(S["xT_ready"], m)
                for t in range(NT):
                    V.tensor_scalar(xn[:, t, :], x_sb[:, g * NT + t, :], mv[:, t, 0:1], rstd[:, t:t + 1],
                                    ALU.subtract, ALU.mult).then_inc(S["xn_ready"], 1)

            def low_of_xT(m, dst):
                dve.wait_ge(S["xh_ready"], m + 1)
                low(dst[1][:, :], ba[:, :], dst[0][:, :], "xl_ready")

            def residual_attention(n):
                g = n % 2
                dve.wait_ge(S["att_ready"], n + 1)
                dve.wait_ge(S["tg_done"], 1)
                xv = x_sb[:, g * NT:(g + 1) * NT, :].rearrange("p t d -> p (t d)")
                V.scalar_tensor_tensor(xv, ba[:, :], tg[:, n // 2:n // 2 + 1], xv, ALU.mult, ALU.add)\
                    .then_inc(S["x_att"], 1)
                dve.wait_ge(S["x_att"], n + 1)

            def route_tokens(n):
                own = 3 * n
                dve.wait_ge(S["logit_ready"], n + 1)
                if n >= 2:
                    pass
                V.tensor_copy(logit[:, :, :].rearrange("p t e -> p (t e)"), bs[:, 0:NT * E]).then_inc(S["logit_sb"], 1)
                dve.wait_ge(S["logit_sb"], 5 * n + 1)
                V.tensor_reduce(lmax[:, :], logit[:, :, :], AX.X, ALU.max).then_inc(S["router_dve"], 1)
                mine = logit[:, :, :].unsqueeze(3).to_broadcast([P, NT, E, E])
                for t in range(NT):
                    other_t = logit[:, t, :].unsqueeze(1).to_broadcast([P, E, E])
                    mine_t = logit[:, t, :].unsqueeze(2).to_broadcast([P, E, E])
                    V.tensor_tensor(cmp_gt[:, t], other_t, mine_t, ALU.is_gt)
                    last = V.tensor_tensor(cmp_eq[:, t], other_t, mine_t, ALU.is_equal)
                last.then_inc(S["logit_sb"], 1)
                dve.wait_ge(S["router_dve"], own + 1)
                V.tensor_tensor(ldiff[:, :, :], logit[:, :, :], lmax[:, :].unsqueeze(2).to_broadcast([P, NT, E]),
                                ALU.subtract).then_inc(S["router_dve"], 1)
                dve.wait_ge(S["logit_sb"], 5 * n + 2)
                V.tensor_tensor(cmp_eq[:, :, :, :].rearrange("p t a b -> p t (a b)"),
                                cmp_eq[:, :, :, :].rearrange("p t a b -> p t (a b)"),
                                before[:, :, :].rearrange("p a b -> p (a b)").unsqueeze(1)
                                .to_broadcast([P, NT, E * E]), ALU.mult).then_inc(S["logit_sb"], 1)
                dve.wait_ge(S["logit_sb"], 5 * n + 3)
                V.tensor_tensor(cmp_gt[:, :, :, :].rearrange("p t a b -> p (t a b)"),
                                cmp_gt[:, :, :, :].rearrange("p t a b -> p (t a b)"),
                                cmp_eq[:, :, :, :].rearrange("p t a b -> p (t a b)"), ALU.add).then_inc(S["logit_sb"], 1)
                dve.wait_ge(S["logit_sb"], 5 * n + 4)
                V.tensor_reduce(rank[:, :, :].rearrange("p t e -> p (t e)"),
                                cmp_gt[:, :, :, :].rearrange("p t a b -> p (t a) b"), AX.X, ALU.add)\
                    .then_inc(S["logit_sb"], 1)
                dve.wait_ge(S["logit_sb"], 5 * n + 5)
                dve.wait_ge(S["lexp_ready"], n + 1)
                V.scalar_tensor_tensor(lsel[:, :, :].rearrange("p t e -> p (t e)"),
                                       rank[:, :, :].rearrange("p t e -> p (t e)"), 2.0,
                                       lexp[:, :, :].rearrange("p t e -> p (t e)"), ALU.is_lt, ALU.mult)\
                    .then_inc(S["router_dve"], 1)
                dve.wait_ge(S["router_dve"], own + 3)
                V.tensor_reduce(lsum[:, :], (lexp if n < 2 else lsel)[:, :, :], AX.X, ALU.add).then_inc(S["route_ready"], 1)
                dve.wait_ge(S["route_ready"], 3 * n + 1)
                V.reciprocal(lrec[:, :], lsum[:, :]).then_inc(S["route_ready"], 1)
                dve.wait_ge(S["route_ready"], 3 * n + 2)
                V.tensor_tensor(route[n % 2][:, :, :], lsel[:, :, :], lrec[:, :].unsqueeze(2).to_broadcast([P, NT, E]),
                                ALU.mult).then_inc(S["route_ready"], 1)

            def attention(n, k):
                g = n % 2
                if n < 2:
                    if k == 0:
                        dve.wait_ge(S[f"ld_x{g}"], 16)
                        normalise(2 * n, g)
                    if k == 1:
                        low_of_xT(2 * n, xa)
                    if k == 2:
                        for h in range(2):
                            dve.wait_ge(S["qh_ready"], 2 * n + h + 1)
                            low(qfs[1][:, h, :], qf[:, h, :], qfs[0][:, h, :], "ql_ready")
                    if 3 <= k < 3 + NT:
                        t = k - 3
                        i = NT * n + t
                        s = bs[:, :].rearrange("p (h k) -> p h k", k=KEYS)
                        dve.wait_ge(S["score_ready"], i + 1)
                        V.tensor_reduce(nmax[:, t, :], s, AX.X, ALU.max, negate=True).then_inc(S["nmax_ready"], 1)
                        dve.wait_ge(S["nmax_ready"], i + 1)
                        if n:
                            dve.wait_ge(S["probT_ready"], NT * (n - 1) + t + 1)
                        V.tensor_tensor(prob[:, t, :].rearrange("p (h k) -> p h k", k=KEYS), s,
                                        nmax[:, t, :].unsqueeze(2).to_broadcast([P, HEADS, KEYS]), ALU.add)\
                            .then_inc(S["shifted"], 1)
                    if k == 7:
                        for t in range(NT):
                            i = NT * n + t
                            dve.wait_ge(S["exp_ready"], i + 1)
                            V.tensor_reduce(psum_[:, t, :], prob[:, t, :].rearrange("p (h k) -> p h k", k=KEYS),
                                            AX.X, ALU.add).then_inc(S["sum_ready"], 1)
                            dve.wait_ge(S["sum_ready"], i + 1)
                            V.reciprocal(prec[:, t, :], psum_[:, t, :]).then_inc(S["rec_ready"], 1)
                    if k == 12:
                        residual_attention(n)
                        normalise(2 * n + 1, g)
                    if k == 13:
                        low_of_xT(2 * n + 1, xf[g])
                    if k == 14:
                        route_tokens(n)
                else:
                    if k == 0:
                        dve.wait_ge(S["x_ffn"], n - 1)
                        normalise(2 * n, g)
                    if k == 1:
                        low_of_xT(2 * n, xa)
                    if k == 2:
                        s = bs[:, 0:NT * KEYS].rearrange("p (t k) -> p t k", k=KEYS)
                        pr = prob1[:, :, 0:KEYS]
                        dve.wait_ge(S["s1_ready"], n - 1)
                        V.tensor_reduce(nmax1[:, :], s, AX.X, ALU.max, negate=True).then_inc(S["s1_nmax"], 1)
                        dve.wait_ge(S["s1_nmax"], n - 1)
                        if n == 3:
                            dve.wait_ge(S["s1_T"], 1)
                        V.tensor_tensor(pr, s, nmax1[:, :].unsqueeze(2).to_broadcast([P, NT, KEYS]), ALU.add)\
                            .then_inc(S["s1_shift"], 1)
                        dve.wait_ge(S["s1_exp"], n - 1)
                        V.tensor_reduce(sum1[:, :], pr, AX.X, ALU.add).then_inc(S["s1_sum"], 1)
                        dve.wait_ge(S["s1_sum"], n - 1)
                        V.reciprocal(rec1[:, :], sum1[:, :]).then_inc(S["s1_rec"], 1)
                        dve.wait_ge(S["s1_rec"], n - 1)
                        V.tensor_tensor(pr, pr, rec1[:, :].unsqueeze(2).to_broadcast([P, NT, KEYS]), ALU.mult)\
                            .then_inc(S["s1_prob"], 1)
                    if k == 5:
                        residual_attention(n)
                        normalise(2 * n + 1, g)
                    if k == 6:
                        low_of_xT(2 * n + 1, xf[g])
                    if k == 7:
                        route_tokens(n)

            def experts(n, k):
                layer, g, ff = n // 2, n % 2, FF[n // 2]
                if k == 0:
                    dve.wait_ge(S["route_ready"], 3 * (n + 1))
                if k < MM1_STEPS:
                    e = k // 2
                    for i in range(2):
                        t = 2 * (k % 2) + i
                        y = 2 * (MM1_STEPS * n + k) + i
                        dve.wait_ge(S["act_ready"], y + 1)
                        if k % 2 == 0 and i == 0 and n:
                            if e >= HID_EXPERTS[layer]:
                                dve.wait_ge(S["hidT_ready"], chunks_before(n) + 2 * (e - HID_EXPERTS[layer] + 1))
                            elif e == 0:
                                dve.wait_ge(S["hidT_ready"], chunks_before(n))
                        V.scalar_tensor_tensor(hid[:, t, e % HID_EXPERTS[layer] * ff:(e % HID_EXPERTS[layer] + 1) * ff], act_sb[:, y % NA, 0:ff],
                                               route[g][:, t, e:e + 1], yb[y % NY][:, ff:2 * ff],
                                               ALU.mult, ALU.mult).then_inc(S["hid_ready"], 1)
                if k in TSTEP[layer]:
                    c = chunks_before(n) + TSTEP[layer].index(k)
                    dve.wait_ge(S["hidh_ready"], c + 1)
                    low(hid_t[1][:, c % 2, :], tb[:, :], hid_t[0][:, c % 2, :], "hidl_ready")
                if k == TAIL[layer] + 1:
                    dve.wait_ge(S["oT_ready"], n + 1)
                    xv = x_sb[:, g * NT:(g + 1) * NT, :].rearrange("p t d -> p (t d)")
                    V.scalar_tensor_tensor(xv, ob[:, :], tg[:, 2 + layer:3 + layer], xv, ALU.mult, ALU.add)\
                        .then_inc(S["x_ffn"], 1)

            key_blocks_at = (0, 0)
            for kind, n, k in SLOTS:
                if kind == "A":
                    attention(n, k)
                    if (n, k) == key_blocks_at:
                        key_blocks()
                    if (n, k) == (0, 2):
                        prepare_values()
                    if (n, k) == (0, 10):
                        prepare_layer1()
                elif kind == "F":
                    experts(n, k)

        @block.tensor
        def _(pe):
            T = nc.tensor

            def product3(out, a, b, start=True, stop=True):
                T.matmul(out, a[0], b[0], start=start, stop=False)
                T.matmul(out, a[0], b[1], start=False, stop=False)
                return T.matmul(out, a[1], b[0], start=False, stop=stop)

            pe.wait_ge(S["const_ready"], 1)
            pe.wait_ge(S["ld_ctx"], 16)
            T.transpose(ba[:, 0:NG * KEYS], ctx_sb[:, :], ident[0:NG * KEYS, 0:NG * KEYS]).then_inc(S["ctxT_done"], 1)
            pe.wait_ge(S["const_ready"], 4)
            pe.wait_ge(S["ld_fm"], 32)
            T.matmul(bs[:, 128:384], rep[:, :], fm_t[:, :].unsqueeze(1).to_broadcast([HD, 32, HD]),
                     start=True, stop=True).then_inc(S["wzp_done"], 1)
            pe.wait_ge(S["wz_done"], 1)
            T.matmul(bs[:, 0:1], rep_sgn[:, :], fm_b[:, :], start=True, stop=True).then_inc(S["bz_done"], 1)
            pe.wait_ge(S["ctxT_sb"], 1)
            for g in range(2):
                last = T.matmul(bp[:, g * NG * KEYS:(g + 1) * NG * KEYS], wz[:, g, :], ctx_t[:, :], start=True, stop=True)
            last.then_inc(S["zk_done"], 1)

            def fc_transposes():
                pe.wait_ge(S["fcp_done"], 2)
                for g in range(2):
                    last = T.transpose(ob[:, g * D:(g + 1) * D], fc_p[:, g].rearrange("n s h e -> n (s h e)"), ident[:, :])
                last.then_inc(S["fcT_done"], 1)

            def values_through_fc():
                pe.wait_ge(S["fcl_done"], 1)
                pe.wait_ge(S["kbdl_done"], 4)
                pe.wait_ge(S["kbdh_done"], 4)
                for b in range(NG):
                    for c in range(4):
                        rows = [kb[:, b, c // 2].rearrange("p h k -> p (h k)")[:, (c % 2) * P:(c % 2) * P + P] for kb in kbd]
                        last = product3(yb[b][:, c * D:(c + 1) * D], rows, [f[:, c // 2, :] for f in fcs])
                    last.then_inc(S["v0_done"], 1)

            def layer1_products(i):
                if i == 0:
                    pe.wait_ge(S["ld_at"], 16 * 6)
                    b = yb[2]
                    T.transpose(b[:, 0:D], wo[:, :], ident[:, :])
                    T.matmul(b[:, D:2 * D], wk[:, :], wq[:, :], start=True, stop=True)
                    T.matmul(b[:, 2 * D:2 * D + 1], wk[:, :], bq[:, :], start=True, stop=True).then_inc(S["l1_pe"], 1)
                elif i == 1:
                    pe.wait_ge(S["l1_sb"], 1)
                    T.matmul(tb[:, 0:D], wv[:, :], wo_t[:, :], start=True, stop=True)
                    T.matmul(tb[0:1, D:2 * D], bv[:, :], wo_t[:, :], start=True, stop=True)
                    T.matmul(tb[:, 256:256 + NG * KEYS], kq[:, :], ctx_t[:, :], start=True, stop=True)
                    T.matmul(tb[0:1, 384:384 + NG * KEYS], bqk[:, :], ctx_t[:, :], start=True, stop=True)\
                        .then_inc(S["l1_pe"], 1)
                else:
                    pe.wait_ge(S["l1_sb"], 2)
                    pe.wait_ge(S["v0_sb"], 2)
                    for b in range(NG):
                        o = ob[0:KEYS, b * D:(b + 1) * D]
                        T.matmul(o, ctx_t[:, b * KEYS:(b + 1) * KEYS], vo[:, :], start=True, stop=False)
                        last = T.matmul(o, ones[:, 0:KEYS], bvo[:, :], start=False, stop=True)
                    last.then_inc(S["l1_pe"], 1)

            def transpose_x(m):
                pe.wait_ge(S["xn_ready"], NT * (m + 1))
                if m:
                    pe.wait_ge(S["xl_ready"], m)
                for t in range(NT):
                    last = T.transpose(ba[:, t * P:(t + 1) * P], xn[:, t, :], ident[:, :])
                last.then_inc(S["xT_ready"], 1)

            def router(n):
                pe.wait_ge(S["xl_ready"], 2 * n + 2)
                pe.wait_ge(S["xh_ready"], 2 * n + 2)
                pe.wait_ge(S["rw_l"], 1)
                for t in range(NT):
                    last = product3(bs[:, t * E:(t + 1) * E], [a[:, t * P:(t + 1) * P] for a in xf[n % 2]],
                                    [r[:, n // 2, :] for r in rws])
                last.then_inc(S["logit_ready"], 1)

            def attention(n, k):
                g = n % 2
                if n < 2:
                    if k == 1:
                        transpose_x(2 * n)
                    if k == 2:
                        pe.wait_ge(S["xl_ready"], 2 * n + 1)
                        pe.wait_ge(S["wzl_done"], 1)
                        pe.wait_ge(S["fk_done"], 1)
                        if n:
                            pe.wait_ge(S["logit_sb"], 5 * (n - 1) + 1)
                        for h in range(2):
                            product3((bs, bp)[h][:, :], [w[:, h, :] for w in wzs], [a[:, :] for a in xa])\
                                .then_inc(S["z_ready"], 1)
                    if 3 <= k < 3 + NT:
                        t = k - 3
                        i = NT * n + t
                        if t == 0:
                            pe.wait_ge(S["kbdh_done"], 4)
                            pe.wait_ge(S["kbdl_done"], 4)
                            pe.wait_ge(S["ql_ready"], 2 * n + 2)
                        else:
                            pe.wait_ge(S["shifted"], i)
                        for h in range(2):
                            last = product3(bs[:, h * 256:(h + 1) * 256],
                                            [q[:, h, t * P:(t + 1) * P] for q in qfs],
                                            [kb[:, g, h].rearrange("p h k -> p (h k)") for kb in kbd])
                        last.then_inc(S["score_ready"], 1)
                    if 9 <= k < 9 + NT:
                        t = k - 9
                        pe.wait_ge(S["probT_sb"], NT * n + t + 1)
                        pe.wait_ge(S["v0_sb"], 2)
                        o = ba[:, t * D:(t + 1) * D]
                        T.matmul(o, ones[:, :], fcb[:, :], start=True, stop=False)
                        for c in range(4):
                            last = T.matmul(o, prob_t[:, t % 2, c, :], v0[:, g, c, :], start=False, stop=(c == 3))
                        if t == NT - 1:
                            last.then_inc(S["att_ready"], 1)
                    if 8 <= k < 8 + NT:
                        t = k - 8
                        pe.wait_ge(S["prob_ready"], NT * n + t + 1)
                        if t:
                            pe.wait_ge(S["probT_sb"], NT * n + t)
                        for c in range(4):
                            last = T.transpose(bp[:, c * P:(c + 1) * P], prob[:, t, c * P:(c + 1) * P], ident[:, :])
                        last.then_inc(S["probT_ready"], 1)
                    if k == 13:
                        transpose_x(2 * n + 1)
                    if k == 14:
                        router(n)
                else:
                    if k == 1:
                        transpose_x(2 * n)
                    if k == 2:
                        pe.wait_ge(S["xl_ready"], 2 * n + 1)
                        pe.wait_ge(S["l1_sb"], 4)
                        pe.wait_ge(S["logit_sb"], 5 * (n - 1) + 1)
                        for t in range(NT):
                            o = bs[:, t * KEYS:(t + 1) * KEYS]
                            product3(o, [a[:, t * P:(t + 1) * P] for a in xa],
                                     [m[:, g * KEYS:(g + 1) * KEYS] for m in m1s], stop=False)
                            last = T.matmul(o, ones[:, :], c1[:, g * KEYS:(g + 1) * KEYS], start=False, stop=True)
                        last.then_inc(S["s1_ready"], 1)
                    if k == 3:
                        pe.wait_ge(S["s1_prob"], n - 1)
                        pe.wait_ge(S["one_col"], 1)
                        for t in range(NT):
                            last = T.transpose(bp[0:KEYS + 1, t * P:(t + 1) * P], prob1[:, t, :], ident[:, :])
                        last.then_inc(S["s1_T"], 1)
                    if k == 4:
                        pe.wait_ge(S["s1_T_sb"], n - 1)
                        pe.wait_ge(S["ld_bo"], 32)
                        for t in range(NT):
                            last = T.matmul(ba[:, t * D:(t + 1) * D], prob1_t[:, t, :], v1[:, g, :], start=True, stop=True)
                        last.then_inc(S["att_ready"], 1)
                    if k == 6:
                        transpose_x(2 * n + 1)
                    if k == 7:
                        router(n)

            def experts(n, k):
                layer, g, ff = n // 2, n % 2, FF[n // 2]
                if k < MM1_STEPS:
                    e = k // 2
                    w = [v[:, e, :, :].rearrange("p s f -> p (s f)") for v in (wa_h[layer], wa_l[layer])]
                    if k == 0:
                        pe.wait_ge(S["xh_ready"], 2 * n + 2)
                        pe.wait_ge(S["xl_ready"], 2 * n + 2)
                    pe.wait_ge(S["wsplit_h"], wa_pieces(layer, e))
                    pe.wait_ge(S["wsplit_l"], wa_pieces(layer, e))
                    for i in range(2):
                        t = 2 * (k % 2) + i
                        y = 2 * (MM1_STEPS * n + k) + i
                        if y >= NY:
                            pe.wait_ge(S["hid_ready"], y - NY + 1)
                        elif y < 2:
                            pe.wait_ge(S["v0_sb"], y + 1)
                        else:
                            pe.wait_ge(S["l1_sb"], 1)
                        product3(yb[y % NY][:, 0:2 * ff], [a[:, t * P:(t + 1) * P] for a in xf[g]], w)\
                            .then_inc(S["y_ready"], 1)
                if k - 1 in TSTEP[layer]:
                    i = TSTEP[layer].index(k - 1)
                    c = chunks_before(n) + i
                    pe.wait_ge(S["hidh_ready"], c + 1)
                    pe.wait_ge(S["hidl_ready"], c + 1)
                    pe.wait_ge(S["wsplit_l"], wb_pieces(layer, i))
                    if i == 0:
                        if n:
                            pe.wait_ge(S["x_ffn"], n)
                        else:
                            pe.wait_ge(S["l1_sb"], 4)
                    product3(ob[:, :], [w[:, i, :] for w in (wb_h[layer], wb_l[layer])],
                             [h[:, c % 2, :] for h in hid_t], start=(i == 0), stop=(i == NCH[layer] - 1))\
                        .then_inc(S["mm2_done"], 1)
                if k in TSTEP[layer]:
                    i = TSTEP[layer].index(k)
                    c = chunks_before(n) + i
                    last_expert = (i * P + P - 1) // ff
                    pe.wait_ge(S["hid_ready"], 2 * MM1_STEPS * n + NT * (last_expert + 1))
                    if c:
                        pe.wait_ge(S["hidl_ready"], c)
                    col = i * P % (HID_EXPERTS[layer] * ff)
                    for t in range(NT):
                        last = T.transpose(tb[:, t * P:(t + 1) * P], hid[:, t, col:col + P], ident[:, :])
                    last.then_inc(S["hidT_ready"], 1)
                if k == TAIL[layer] + 1:
                    pe.wait_ge(S["o_sb"], n + 1)
                    for t in range(NT):
                        last = T.transpose(ob[:, t * P:(t + 1) * P], o_t[:, t * P:(t + 1) * P], ident[:, :])
                    last.then_inc(S["oT_ready"], 1)

            for kind, n, k in SLOTS:
                if kind == "A":
                    attention(n, k)
                    if (n, k) == (0, 2):
                        fc_transposes()
                        values_through_fc()
                    if n == 0 and k in (9, 10, 11):
                        layer1_products(k - 9)
                elif kind == "F":
                    experts(n, k)


_INS = ['x', 'ctx_1024', 'g_xattn', 'g_ffn', 'L0_xattn_fm_w', 'L0_xattn_fm_b', 'L0_xattn_fc_w', 'L0_xattn_fc_b',
        'L0_ffn_router_weight', 'L0_ffn_w1', 'L0_ffn_w2', 'L1_xattn_Wk', 'L1_xattn_Wv', 'L1_xattn_bv',
        'L1_xattn_Wq', 'L1_xattn_bq', 'L1_xattn_Wo', 'L1_xattn_bo', 'L1_ffn_w_gate', 'L1_ffn_w1', 'L1_ffn_w3',
        'L1_ffn_w2']


def kernel(**inputs):
    import numpy as _np
    import concourse.bacc as _bacc
    from concourse import mybir as _mybir
    from concourse.bass_utils import run_bass_kernel_spmd as _run

    nc = _bacc.Bacc("TRN2", target_bir_lowering=False, num_devices=1)
    arrays, args = {}, []
    for name in _INS:
        a = _np.ascontiguousarray(inputs[name])
        arrays[f"in_{name}_dram"] = a
        args.append(nc.dram_tensor(f"in_{name}_dram", a.shape, _mybir.dt.from_np(a.dtype), kind="ExternalInput").ap())
    args.append(nc.dram_tensor("out_0_dram", (2, 512, 128), _mybir.dt.float32, kind="ExternalOutput").ap())
    build(nc, *args)
    r = _run(nc, [arrays], core_ids=[0])
    return r.results[0]["out_0_dram"]
```

```python
import concourse.bass as bass
from concourse import mybir
from contextlib import ExitStack

P = 128
D = 128
TOK = 512
NT = TOK // P
NG = 2
KEYS = 32
HEADS, HD = 16, 8
HG = 8
E = 8
FF = (176, 256)
NCH = tuple(E * f // P for f in FF)
EPS = 1e-5
SCALE = 1.0 / float(D) ** 0.5
NY = 4

NA = 4
HID_EXPERTS = (8, 3)

MM1_STEPS = 2 * E


def chunk_steps(layer):
    steps = []
    for c in range(NCH[layer]):
        last_expert = (c * P + P - 1) // FF[layer]
        steps.append(max(2 * last_expert + 2, steps[-1] + 1 if steps else 0))
    return steps


TSTEP = (chunk_steps(0), chunk_steps(1))
TAIL = tuple(s[-1] + 2 for s in TSTEP)
F_STEPS = tuple(t + 2 for t in TAIL)
A_STEPS = (20, 11)
WPIECES = 18


def chunks_before(n):
    return sum(NCH[m // 2] for m in range(n))


def order_of_norm(n, which):
    return 2 * which + n if n < 2 else 2 * n + which


A_LAG = 6
A1_OFFSETS = (0, 1, 2, 3, 4, 5, 6, 7, 8, 9, 10)


def slots():
    last_out = A_LAG + 15
    f_start = [last_out + 1]
    for n in range(3):
        f_start.append(f_start[n] + MM1_STEPS + 2)
    table = [([], [], [], []) for _ in range(f_start[3] + F_STEPS[1])]
    for n in range(4):
        for k in range(F_STEPS[n // 2]):
            table[f_start[n] + k][0].append((n, k))
    for n in range(2):
        for k in range(A_STEPS[0]):
            table[A_LAG * n + k][1].append((n, k))
    for n in range(2, 4):
        start = f_start[n - 2] + F_STEPS[0]
        assert start + A1_OFFSETS[-1] < f_start[n]
        for k, at in enumerate(A1_OFFSETS):
            table[start + at][1].append((n, k))
    for i, at in enumerate([3, 4, 5, 6, 8, 9] + [f_start[0] + i for i in range(WPIECES - 6)]):
        table[at][2].append(i)
    for i, at in enumerate((5, 7, 9)):
        table[f_start[0] + at][3].append(i)
    return table


SLOTS = slots()
VALUES_AT = (0, 7)


def build(nc, x_d, ctx_d, gx_d, gf_d, fmw_d, fmb_d, fcw_d, fcb_d, rw0_d, w1_d, w2_d,
          wk_d, wv_d, bv_d, wq_d, bq_d, wo_d, bo_d, rw1_d, u1_d, u3_d, u2_d, out_d):
    f32, f32r = mybir.dt.float32, mybir.dt.float32r
    ALU, ACT, AX = mybir.AluOpType, mybir.ActivationFunctionType, mybir.AxisListType
    stack = ExitStack()
    with stack:
        def sb(name, shape, dt=f32):
            return stack.enter_context(nc.sbuf_tensor(name, shape, dt))

        def sem(name):
            return stack.enter_context(nc.semaphore(name))

        x_sb = sb("x_sb", [P, NG * NT, D])
        stats = sb("stats", [P, NT, 6])
        mv = sb("mv", [P, NT, 2])
        rstd = sb("rstd", [P, NT])
        varp = sb("varp", [P, NT])
        half = sb("half", [P, NT])
        xn = sb("xn", [P, NT, D])
        xa = [sb(f"xa{i}", [P, TOK], f32r) for i in "hl"]
        xf = [[sb(f"xf{g}{i}", [P, TOK], f32r) for i in "hl"] for g in range(NG)]

        ident = sb("ident", [P, P])
        ones = sb("ones", [1, P])
        sgn_mask = sb("sgn_mask", [P, 2, 2, HG * HD])
        key_mask = sb("key_mask", [P, HG, KEYS])
        rep = sb("rep", [HD, P])
        rep_sgn = sb("rep_sgn", [HD, P])
        fm_t = sb("fm_t", [HD, HD])
        fm_b = sb("fm_b", [HD, 1])
        wz = sb("wz", [P, 2, P])
        wzs = [sb(f"wz{i}", [P, 2, P], f32r) for i in "hl"]
        bz = sb("bz", [P, 1])
        ctx_sb = sb("ctx_sb", [NG * KEYS, D])
        ctx_t = sb("ctx_t", [D, NG * KEYS])
        fk = sb("fk", [P, 2, NG * KEYS])
        fks = [sb(f"fk{i}", [P, 2, NG * KEYS], f32r) for i in "hl"]
        kbd = [sb(f"kbd{i}", [P, NG, 2, HG, KEYS], f32r) for i in "hl"]
        fcs = [sb(f"fc{i}", [P, 2, D], f32r) for i in "hl"]
        fcb = sb("fcb", [1, D])
        v0 = sb("v0", [P, NG, 4, D])
        gates = sb("gates", [P, 4])
        tg = sb("tg", [P, 4])

        wq, wk, wv, wo = (sb(n, [D, D]) for n in ("wq", "wk", "wv", "wo"))
        bq, bv = sb("bq", [D, 1]), sb("bv", [D, 1])
        wo_t = sb("wo_t", [D, D])
        kq = sb("kq", [D, D])
        vo = sb("vo", [D, D])
        bqk = sb("bqk", [D, 1])
        bvo = sb("bvo", [1, D])
        m1s = [sb(f"m1{i}", [D, NG * KEYS], f32r) for i in "hl"]
        c1 = sb("c1", [1, NG * KEYS])
        v1 = sb("v1", [KEYS + 1, NG, D])

        qfs = [sb(f"qf{i}", [P, 2, TOK], f32r) for i in "hl"]
        nmax = sb("nmax", [P, NT, HEADS])
        hid = sb("hid", [P, NT, NCH[0] * P])
        prob = [sb("prob", [P, NT, HEADS * KEYS])[:, :, :], hid[:, :, 0:HEADS * KEYS]]
        qf = [p[:, 0:2, :] for p in prob]
        fc_sb = hid[:, 0, 512:768].rearrange("n (g h s e) -> n g h s e", g=2, h=HG, s=2)
        fc_p = hid[:, 0, 768:1024].rearrange("n (g s h e) -> n g s h e", g=2, s=2, h=HG)
        psum_ = sb("psum_", [P, NT, HEADS])
        prec = sb("prec", [P, NT, HEADS])
        prob_t = sb("prob_t", [P, 2, 4, P])
        prob1 = sb("prob1", [P, NT, KEYS + 1])
        nmax1, sum1, rec1 = sb("nmax1", [P, NT]), sb("sum1", [P, NT]), sb("rec1", [P, NT])
        prob1_t = sb("prob1_t", [KEYS + 1, NT, P])

        rw = sb("rw", [D, 2, E])
        rws = [sb(f"rw{i}", [D, 2, E], f32r) for i in "hl"]
        logit = sb("logit", [P, NT, E])
        before = sb("before", [P, E, E])
        cmp_gt = xn[:, 0:2, :].rearrange("p a (b i j) -> p (a b) i j", i=E, j=E)
        cmp_eq = xn[:, 2:4, :].rearrange("p a (b i j) -> p (a b) i j", i=E, j=E)
        rank = sb("rank", [P, NT, E])
        lmax = sb("lmax", [P, NT])
        ldiff = sb("ldiff", [P, NT, E])
        lexp = sb("lexp", [P, NT, E])
        lsel = sb("lsel", [P, NT, E])
        lsum, lrec = sb("lsum", [P, NT]), sb("lrec", [P, NT])
        route = [sb(f"route{g}", [P, NT, E]) for g in range(NG)]

        stage = sb("stage", [P, 2 * E * FF[0] + NCH[0] * P])
        wa_f = [stage[:, 0:2 * E * ff].rearrange("p (e s f) -> p e s f", e=E, s=2) for ff in FF]
        wb_f = [stage[:, 2 * E * FF[0]:].rearrange("p (c n) -> p c n", n=D),
                stage[:, 0:NCH[1] * D].rearrange("p (c n) -> p c n", n=D)]
        wa_l = [sb(f"wal{l}", [D, E, 2, FF[l]], f32r) for l in range(2)]
        wa_h = [sb(f"wah{l}", [D, E, 2, FF[l]], f32r) for l in range(2)]
        wb_h = [sb(f"wbh{l}", [P, NCH[l], D], f32r) for l in range(2)]
        wb_l = [sb(f"wbl{l}", [P, NCH[l], D], f32r) for l in range(2)]
        act_sb = sb("act_sb", [P, NA, FF[1]])
        hid_t = [sb(f"hid_t{i}", [P, 2, TOK], f32r) for i in "hl"]
        o_t = sb("o_t", [D, TOK])

        bank = [stack.enter_context(nc.psum_tensor(f"bank{i}", [P, 512], f32)) for i in range(8)]
        yb, tb, ob = bank[0:NY], bank[4], bank[5]
        bs, bp = bank[6], bank[7]

        names = """ld_x0 ld_x1 ld_ctx ld_fm ld_fc ld_g ld_r ld_at ld_bo ld_w0 ld_w1 ld_w2 ld_w3 ld_w4 ld_w5 ld_w6 ld_w7 ld_w8 ld_w9 out_done
            const_ready pool_own rstd_ready var_ready
            wzp_done wz_done wzh_done wzl_done bz_done ctxT_done ctxT_sb zk_done fk_done fkh_done fkl_done
            kbdh_done kbdl_done fcp_done fcT_done fch_done fcl_done v0_done v0_sb tg_done
            l1_pe l1_sb one_col rw_h rw_l
            stats_ready mv_ready xn_ready xT_ready xh_ready xl_ready
            z_ready qf_ready qh_ready ql_ready score_ready nmax_ready shifted exp_ready sum_ready rec_ready
            prob_ready probT_ready probT_sb att_ready x_att
            s1_ready s1_nmax s1_shift s1_exp s1_sum s1_rec s1_prob s1_T s1_T_sb
            logit_ready logit_sb router_dve lexp_ready route_ready
            wsplit_h wsplit_l
            y_ready act_ready hid_ready hidT_ready hidh_ready hidl_ready mm2_done o_sb oT_ready x_ffn"""
        S = {n: sem(n) for n in names.split()}

        block = stack.enter_context(nc.Block())

        score_b = [(bs, yb[2]), (yb[0], yb[3])]
        main_b = [bs, yb[0], bs, bs]
        prob_b = [bp, yb[1], bp, bp]

        def flat(t):
            return t.rearrange("p e s f -> p e (s f)")

        pieces = []
        for q in range(4):
            pieces.append([v[:, 2 * q:2 * q + 2, :] for v in (flat(wa_f[0]), flat(wa_h[0][:, :, :, :]), flat(wa_l[0][:, :, :, :]))])
        for a, b in ((0, 6), (6, NCH[0])):
            pieces.append([v[:, a:b, :] for v in (wb_f[0], wb_h[0], wb_l[0])])
        for q in range(8):
            pieces.append([v[:, q:q + 1, :] for v in (flat(wa_f[1]), flat(wa_h[1][:, :, :, :]), flat(wa_l[1][:, :, :, :]))])
        for q in range(4):
            pieces.append([v[:, 4 * q:4 * q + 4, :] for v in (wb_f[1], wb_h[1], wb_l[1])])
        assert len(pieces) == WPIECES
        load_of = [0, 1, 2, 3, 4, 4] + [5, 5, 6, 6, 7, 7, 8, 8] + [9] * 4
        landed = [32 if 5 <= i <= 8 else 16 for i in load_of]
        def wa_pieces(layer, e):
            return e // 2 + 1 if layer == 0 else 6 + e + 1

        def wb_pieces(layer, c):
            return (5 if c < 6 else 6) if layer == 0 else 14 + c // 4 + 1

        @block.sync
        def _(sp):
            def load(dst, src, s):
                sp.dma_start(dst, src).then_inc(S[s], 16)
            load(x_sb[:, 0:NT, :], x_d[0].rearrange("(t p) d -> p t d", p=P), "ld_x0")
            load(ctx_sb[:, :], ctx_d.rearrange("b k d -> (b k) d"), "ld_ctx")
            load(fc_sb[:, :, :, :, :], fcw_d.rearrange("n (g h s e) -> n g h s e", g=2, h=HG, s=2), "ld_fc")
            load(fcb[:, :], fcb_d.rearrange("(a n) -> a n", a=1), "ld_fc")
            for q in range(4):
                load(wa_f[0][:, 2 * q:2 * q + 2, :, :].rearrange("p e s f -> p e (s f)"),
                     w1_d[2 * q:2 * q + 2].rearrange("e p f -> p e f"), f"ld_w{q}")
            load(wb_f[0][:, :, :], w2_d.rearrange("e f n -> (e f) n").rearrange("(c p) n -> p c n", p=P), "ld_w4")
            load(x_sb[:, NT:2 * NT, :], x_d[1].rearrange("(t p) d -> p t d", p=P), "ld_x1")
            for i, r in enumerate((rw0_d, rw1_d)):
                load(rw[:, i, :], r, "ld_r")
            for dst, src in ((wq, wq_d), (wk, wk_d), (wv, wv_d), (wo, wo_d)):
                load(dst[:, :], src, "ld_at")
            for dst, src in ((bq, bq_d), (bv, bv_d)):
                load(dst[:, :], src.rearrange("(d a) -> d a", a=1), "ld_at")
            for b in range(NG):
                load(v1[KEYS:KEYS + 1, b, :], bo_d.rearrange("(a n) -> a n", a=1), "ld_bo")
            for q in range(4):
                if q == 0:
                    sp.wait_ge(S["wsplit_l"], 4)
                if q == 2:
                    sp.wait_ge(S["wsplit_l"], 6)
                for s, w in enumerate((u1_d, u3_d)):
                    load(wa_f[1][:, 2 * q:2 * q + 2, s, :], w[2 * q:2 * q + 2].rearrange("e p f -> p e f"), f"ld_w{5 + q}")
            sp.wait_ge(S["wsplit_l"], 10)
            load(wb_f[1][:, :, :], u2_d.rearrange("e f n -> (e f) n").rearrange("(c p) n -> p c n", p=P), "ld_w9")
            for g in range(NG):
                sp.wait_ge(S["x_ffn"], NG + g + 1)
                sp.dma_start(out_d[g].rearrange("(t p) d -> p t d", p=P),
                             x_sb[:, g * NT:(g + 1) * NT, :]).then_inc(S["out_done"], 16)
            sp.wait_ge(S["out_done"], 16 * NG)

        @block.gpsimd
        def _(pool):
            own = [0]

            def step(ins):
                own[0] += 1
                ins.then_inc(S["pool_own"], 1)
                pool.wait_ge(S["pool_own"], own[0])

            def select(ap, pattern, base, cm, op, fill):
                return pool.affine_select(out=ap, in_=ap, compare_op=op, fill=fill, base=base,
                                          pattern=pattern, channel_multiplier=cm)

            step(pool.memset(ident[:, :], 0.0))
            select(ident[:, :], [[-1, P]], 0, 1, ALU.not_equal, 1.0).then_inc(S["const_ready"], 1)
            pool.memset(rep[:, :], 0.0)
            step(pool.memset(rep_sgn[:, :], 0.0))
            select(rep[:, :].rearrange("p (h d) -> p h d", d=HD), [[0, HEADS], [-1, HD]], 0, 1,
                   ALU.not_equal, 1.0).then_inc(S["const_ready"], 1)
            for s, sign in enumerate((1.0, -1.0)):
                select(rep_sgn[:, s * 64:s * 64 + 64].rearrange("p (h d) -> p h d", d=HD), [[0, HG], [-1, HD]], 0, 1,
                       ALU.not_equal, sign).then_inc(S["const_ready"], 1)
            pool.memset(sgn_mask[:, :, 0, :], 1.0)
            step(pool.memset(sgn_mask[:, :, 1, :], -1.0))
            for g in range(2):
                v = sgn_mask[:, g, :, :].rearrange("p s (h e) -> p s h e", e=HD)
                step(select(v, [[0, 2], [-HD, HG], [0, HD]], -64 * g, 1, ALU.is_ge, 0.0))
                select(v, [[0, 2], [HD, HG], [0, HD]], 64 * g + HD - 1, -1, ALU.is_ge, 0.0)\
                    .then_inc(S["const_ready"], 1)
            pool.memset(half[:, :], -0.5)
            pool.memset(ones[:, :], 1.0).then_inc(S["const_ready"], 1)
            step(pool.memset(key_mask[:, :, :], 1.0))
            for r in range(2):
                v = key_mask[64 * r:64 * r + 64, :, :]
                step(select(v, [[-HD, HG], [0, KEYS]], 0, 1, ALU.is_ge, 0.0))
                select(v, [[HD, HG], [0, KEYS]], HD - 1, -1, ALU.is_ge, 0.0).then_inc(S["const_ready"], 1)
                pool.wait_ge(S["const_ready"], 8 + r)
            step(pool.memset(before[:, :, :], 1.0))
            select(before[:, :, :], [[1, E], [-1, E]], 0, 0, ALU.is_gt, 0.0).then_inc(S["const_ready"], 1)
            pool.memset(prob1[:, :, KEYS:KEYS + 1], 1.0).then_inc(S["one_col"], 1)
            pool.wait_ge(S["ld_fc"], 32)
            for g in range(2):
                pool.tensor_copy(fc_p[:, g], fc_sb[:, g].rearrange("n h s e -> n s h e")).then_inc(S["fcp_done"], 1)

            def rstd_of(n, which):
                m = order_of_norm(n, which)
                pool.wait_ge(S["mv_ready"], NT * (m + 1))
                step(pool.tensor_scalar(varp[:, :], mv[:, :, 1], EPS, None, ALU.add))
                pool.tensor_tensor(rstd[:, :], varp[:, :], half[:, :], ALU.pow).then_inc(S["rstd_ready"], 1)

            def attention(n, k):
                if k == 0:
                    rstd_of(n, 0)
                if n < 2:
                    if 10 <= k < 10 + NT:
                        t = k - 10
                        pool.wait_ge(S["rec_ready"], NT * n + t + 1)
                        v = prob[n][:, t, :].rearrange("p (h k) -> p h k", k=KEYS)
                        pool.tensor_tensor(v, v, prec[:, t, :].unsqueeze(2).to_broadcast([P, HEADS, KEYS]),
                                           ALU.mult).then_inc(S["prob_ready"], 1)
                    if k == 15:
                        rstd_of(n, 1)
                elif k == 6:
                    rstd_of(n, 1)

            def split(i):
                full, h, l = pieces[i]
                pool.wait_ge(S["wsplit_h"], i + 1)
                pool.tensor_tensor(l, full, h.bitcast(f32), ALU.subtract).then_inc(S["wsplit_l"], 1)

            for slot, (_, attentions, split_pieces, _) in enumerate(SLOTS):
                for n, k in attentions:
                    attention(n, k)
                for i in split_pieces:
                    split(i)
                if slot == 0:
                    pool.wait_ge(S["fkl_done"], 1)
                    for b in range(NG):
                        for g in range(2):
                            pool.tensor_tensor(kbd[1][:, b, g], key_mask[:, :, :],
                                               fks[1][:, g, b * KEYS:(b + 1) * KEYS].bitcast(f32).unsqueeze(1)
                                               .to_broadcast([P, HG, KEYS]), ALU.mult).then_inc(S["kbdl_done"], 1)

        @block.scalar
        def _(act):
            act.dma_start(fm_t[:, :], fmw_d.rearrange("e d -> d e"), allow_slow_non_contiguous=True)\
                .then_inc(S["ld_fm"], 16)
            act.dma_start(fm_b[:, :], fmb_d.rearrange("(d a) -> d a", a=1)).then_inc(S["ld_fm"], 16)
            for i, g in enumerate((gx_d, gf_d)):
                act.dma_start(gates[:, 2 * i:2 * i + 2], g.rearrange("(a n) -> a n", a=1).to_broadcast([P, 2]))\
                    .then_inc(S["ld_g"], 16)
            def copy(dst, src):
                return nc.scalar.activation(dst, src, ACT.Copy)

            act.wait_ge(S["ctxT_done"], 1)
            copy(ctx_t[:, :], tb[:, 0:NG * KEYS]).then_inc(S["ctxT_sb"], 1)
            act.wait_ge(S["wz_done"], 1)
            copy(wzs[0][:, :, :], wz[:, :, :]).then_inc(S["wzh_done"], 1)
            act.wait_ge(S["bz_done"], 1)
            copy(bz[:, :], bs[:, 0:1]).then_inc(S["bz_done"], 1)
            act.wait_ge(S["zk_done"], 1)
            act.wait_ge(S["bz_done"], 2)
            nc.scalar.activation(fk[:, :, :].rearrange("p g k -> p (g k)"), bp[:, 0:2 * NG * KEYS], ACT.Exp,
                                 bias=bz[:, 0:1]).then_inc(S["fk_done"], 1)
            act.wait_ge(S["fk_done"], 1)
            copy(fks[0][:, :, :], fk[:, :, :]).then_inc(S["fkh_done"], 1)
            act.wait_ge(S["ld_g"], 32)
            nc.scalar.activation(tg[:, :], gates[:, :], ACT.Tanh).then_inc(S["tg_done"], 1)

            def prepare_values():
                act.wait_ge(S["fcT_done"], 1)
                copy(fcs[0][:, :, :].rearrange("p g n -> p (g n)"), tb[:, 0:2 * D]).then_inc(S["fch_done"], 1)
                for b in range(NG):
                    act.wait_ge(S["v0_done"], b + 1)
                    copy(v0[:, b, :, :].rearrange("p c n -> p (c n)"), (ob, tb)[b][:, :]).then_inc(S["v0_sb"], 1)
                act.wait_ge(S["ld_r"], 32)
                copy(rws[0][:, :, :], rw[:, :, :]).then_inc(S["rw_h"], 1)

            def prepare_layer1(i):
                act.wait_ge(S["l1_pe"], i + 1)
                if i == 0:
                    copy(wo_t[:, :], bp[:, 0:D])
                    copy(kq[:, :], bp[:, D:2 * D])
                    copy(bqk[:, :], bp[:, 2 * D:2 * D + 1]).then_inc(S["l1_sb"], 1)
                elif i == 1:
                    copy(vo[:, :], bs[:, 0:D])
                    copy(bvo[:, :], bs[0:1, D:2 * D])
                    copy(m1s[0][:, :], bs[:, 256:256 + NG * KEYS])
                    copy(c1[:, :], bs[0:1, 384:384 + NG * KEYS]).then_inc(S["l1_sb"], 1)
                else:
                    copy(v1[0:KEYS, :, :].rearrange("k b n -> k (b n)"), bp[0:KEYS, 0:NG * D]).then_inc(S["l1_sb"], 1)

            def high_of_xT(n, which, dst):
                act.wait_ge(S["xT_ready"], order_of_norm(n, which) + 1)
                copy(dst[0][:, :], (bs if which else main_b[n])[:, :]).then_inc(S["xh_ready"], 1)

            def router_exp(n):
                act.wait_ge(S["router_dve"], 3 * n + 2)
                nc.scalar.activation(lexp[:, :, :], ldiff[:, :, :], ACT.Exp).then_inc(S["lexp_ready"], 1)

            def attention(n, k):
                g = n % 2
                if k == 2:
                    high_of_xT(n, 0, xa)
                if n < 2:
                    if k == 3:
                        for h in range(2):
                            act.wait_ge(S["z_ready"], 2 * n + h + 1)
                            nc.scalar.activation(qf[n][:, h, :], (main_b[n], prob_b[n])[h][:, :], ACT.Exp,
                                                 bias=bz[:, 0:1]).then_inc(S["qf_ready"], 1)
                        for h in range(2):
                            act.wait_ge(S["qf_ready"], 2 * n + h + 1)
                            if n:
                                act.wait_ge(S["score_ready"], NT)
                            copy(qfs[0][:, h, :], qf[n][:, h, :]).then_inc(S["qh_ready"], 1)
                    if 6 <= k < 6 + NT:
                        t = k - 6
                        act.wait_ge(S["shifted"], NT * n + t + 1)
                        nc.scalar.activation(prob[n][:, t, :], prob[n][:, t, :], ACT.Exp,
                                             scale=SCALE).then_inc(S["exp_ready"], 1)
                    if 11 <= k < 11 + NT:
                        t = k - 11
                        act.wait_ge(S["probT_ready"], NT * n + t + 1)
                        copy(prob_t[:, t % 2].rearrange("p c q -> p (c q)"), prob_b[n][:, :]).then_inc(S["probT_sb"], 1)
                    if k == 17:
                        high_of_xT(n, 1, xf[g])
                    if k == 18:
                        router_exp(n)
                else:
                    if k == 3:
                        act.wait_ge(S["s1_shift"], n - 1)
                        nc.scalar.activation(prob1[:, :, 0:KEYS], prob1[:, :, 0:KEYS], ACT.Exp,
                                             scale=SCALE).then_inc(S["s1_exp"], 1)
                    if k == 5:
                        act.wait_ge(S["s1_T"], n - 1)
                        copy(prob1_t[:, :, :].rearrange("k t q -> k (t q)"), bp[0:KEYS + 1, :]).then_inc(S["s1_T_sb"], 1)
                    if k == 8:
                        high_of_xT(n, 1, xf[g])
                    if k == 9:
                        router_exp(n)

            def silu(n, k, i):
                y = 2 * (MM1_STEPS * n + k) + i
                ff = FF[n // 2]
                act.wait_ge(S["y_ready"], y + 1)
                if y >= NA:
                    act.wait_ge(S["hid_ready"], y - NA + 1)
                nc.scalar.activation(act_sb[:, y % NA, 0:ff], yb[y % NY][:, 0:ff], ACT.Silu)\
                    .then_inc(S["act_ready"], 1)

            def experts(n, k):
                layer = n // 2
                if k < MM1_STEPS:
                    silu(n, k, 0)
                if k in TSTEP[layer]:
                    c = chunks_before(n) + TSTEP[layer].index(k)
                    act.wait_ge(S["hidT_ready"], c + 1)
                    if c >= 2:
                        act.wait_ge(S["mm2_done"], c - 1)
                    copy(hid_t[0][:, c % 2, :], tb[:, :]).then_inc(S["hidh_ready"], 1)
                if k < MM1_STEPS:
                    silu(n, k, 1)
                if k == TAIL[layer]:
                    act.wait_ge(S["mm2_done"], chunks_before(n + 1))
                    copy(o_t[:, :], ob[:, :]).then_inc(S["o_sb"], 1)

            def split(i):
                full, h, l = pieces[i]
                act.wait_ge(S[f"ld_w{load_of[i]}"], landed[i])
                copy(h, full).then_inc(S["wsplit_h"], 1)

            for expert_steps, attentions, split_pieces, parts in SLOTS:
                for n, k in expert_steps:
                    experts(n, k)
                for n, k in attentions:
                    attention(n, k)
                    if (n, k) == VALUES_AT:
                        prepare_values()
                for i in split_pieces:
                    split(i)
                for i in parts:
                    prepare_layer1(i)

        @block.vector
        def _(dve):
            V = nc.vector

            def low(dst, full, high, s):
                V.tensor_tensor(dst, full, high.bitcast(f32), ALU.subtract).then_inc(S[s], 1)

            dve.wait_ge(S["wzp_done"], 1)
            dve.wait_ge(S["const_ready"], 6)
            V.tensor_tensor(wz[:, :, :].rearrange("p g c -> p (g c)"), bs[:, 128:384],
                            sgn_mask[:, :, :, :].rearrange("p g s c -> p (g s c)"), ALU.mult).then_inc(S["wz_done"], 1)
            dve.wait_ge(S["wz_done"], 1)
            dve.wait_ge(S["wzh_done"], 1)
            low(wzs[1][:, :, :], wz[:, :, :], wzs[0][:, :, :], "wzl_done")

            def key_blocks():
                dve.wait_ge(S["fkh_done"], 1)
                low(fks[1][:, :, :], fk[:, :, :], fks[0][:, :, :], "fkl_done")
                dve.wait_ge(S["const_ready"], 10)
                for b in range(NG):
                    for g in range(2):
                        V.tensor_tensor(kbd[0][:, b, g], key_mask[:, :, :],
                                        fks[0][:, g, b * KEYS:(b + 1) * KEYS].bitcast(f32).unsqueeze(1)
                                        .to_broadcast([P, HG, KEYS]), ALU.mult).then_inc(S["kbdh_done"], 1)

            def prepare_values():
                dve.wait_ge(S["fch_done"], 1)
                low(fcs[1][:, :, :].rearrange("p g n -> p (g n)"), tb[:, 0:2 * D],
                    fcs[0][:, :, :].rearrange("p g n -> p (g n)"), "fcl_done")
                dve.wait_ge(S["rw_h"], 1)
                low(rws[1][:, :, :], rw[:, :, :], rws[0][:, :, :], "rw_l")

            def prepare_layer1():
                dve.wait_ge(S["l1_sb"], 2)
                low(m1s[1][:, :], bs[:, 256:256 + NG * KEYS], m1s[0][:, :], "l1_sb")

            def statistics(n, which):
                m, g = order_of_norm(n, which), n % 2
                for t in range(NT):
                    V.bn_stats(stats[:, t, :], x_sb[:, g * NT + t, :]).then_inc(S["stats_ready"], 1)
                for t in range(NT):
                    dve.wait_ge(S["stats_ready"], NT * m + t + 1)
                    V.bn_aggr(mv[:, t, :], stats[:, t, :]).then_inc(S["mv_ready"], 1)

            def normalise(n, which):
                m, g = order_of_norm(n, which), n % 2
                dve.wait_ge(S["rstd_ready"], m + 1)
                if m:
                    dve.wait_ge(S["xT_ready"], m)
                for t in range(NT):
                    V.tensor_scalar(xn[:, t, :], x_sb[:, g * NT + t, :], mv[:, t, 0:1], rstd[:, t:t + 1],
                                    ALU.subtract, ALU.mult).then_inc(S["xn_ready"], 1)

            def low_of_xT(n, which, dst):
                dve.wait_ge(S["xh_ready"], order_of_norm(n, which) + 1)
                low(dst[1][:, :], (bs if which else main_b[n])[:, :], dst[0][:, :], "xl_ready")

            def residual_attention(n):
                g = n % 2
                dve.wait_ge(S["att_ready"], n + 1)
                dve.wait_ge(S["tg_done"], 1)
                xv = x_sb[:, g * NT:(g + 1) * NT, :].rearrange("p t d -> p (t d)")
                V.scalar_tensor_tensor(xv, main_b[n][:, :], tg[:, n // 2:n // 2 + 1], xv, ALU.mult, ALU.add)\
                    .then_inc(S["x_att"], 1)
                dve.wait_ge(S["x_att"], n + 1)

            def route_tokens(n):
                own = 3 * n
                dve.wait_ge(S["logit_ready"], n + 1)
                V.tensor_copy(logit[:, :, :].rearrange("p t e -> p (t e)"), bs[:, 0:NT * E]).then_inc(S["logit_sb"], 1)
                dve.wait_ge(S["logit_sb"], 5 * n + 1)
                V.tensor_reduce(lmax[:, :], logit[:, :, :], AX.X, ALU.max).then_inc(S["router_dve"], 1)
                mine = logit[:, :, :].unsqueeze(3).to_broadcast([P, NT, E, E])
                for t in range(NT):
                    other_t = logit[:, t, :].unsqueeze(1).to_broadcast([P, E, E])
                    mine_t = logit[:, t, :].unsqueeze(2).to_broadcast([P, E, E])
                    V.tensor_tensor(cmp_gt[:, t], other_t, mine_t, ALU.is_gt)
                    last = V.tensor_tensor(cmp_eq[:, t], other_t, mine_t, ALU.is_equal)
                last.then_inc(S["logit_sb"], 1)
                dve.wait_ge(S["router_dve"], own + 1)
                V.tensor_tensor(ldiff[:, :, :], logit[:, :, :], lmax[:, :].unsqueeze(2).to_broadcast([P, NT, E]),
                                ALU.subtract).then_inc(S["router_dve"], 1)
                dve.wait_ge(S["logit_sb"], 5 * n + 2)
                V.tensor_tensor(cmp_eq[:, :, :, :].rearrange("p t a b -> p t (a b)"),
                                cmp_eq[:, :, :, :].rearrange("p t a b -> p t (a b)"),
                                before[:, :, :].rearrange("p a b -> p (a b)").unsqueeze(1)
                                .to_broadcast([P, NT, E * E]), ALU.mult).then_inc(S["logit_sb"], 1)
                dve.wait_ge(S["logit_sb"], 5 * n + 3)
                V.tensor_tensor(cmp_gt[:, :, :, :].rearrange("p t a b -> p (t a b)"),
                                cmp_gt[:, :, :, :].rearrange("p t a b -> p (t a b)"),
                                cmp_eq[:, :, :, :].rearrange("p t a b -> p (t a b)"), ALU.add).then_inc(S["logit_sb"], 1)
                dve.wait_ge(S["logit_sb"], 5 * n + 4)
                V.tensor_reduce(rank[:, :, :].rearrange("p t e -> p (t e)"),
                                cmp_gt[:, :, :, :].rearrange("p t a b -> p (t a) b"), AX.X, ALU.add)\
                    .then_inc(S["logit_sb"], 1)

            def route_weights(n):
                own = 3 * n
                dve.wait_ge(S["logit_sb"], 5 * n + 5)
                dve.wait_ge(S["lexp_ready"], n + 1)
                V.scalar_tensor_tensor(lsel[:, :, :].rearrange("p t e -> p (t e)"),
                                       rank[:, :, :].rearrange("p t e -> p (t e)"), 2.0,
                                       lexp[:, :, :].rearrange("p t e -> p (t e)"), ALU.is_lt, ALU.mult)\
                    .then_inc(S["router_dve"], 1)
                dve.wait_ge(S["router_dve"], own + 3)
                V.tensor_reduce(lsum[:, :], (lexp if n < 2 else lsel)[:, :, :], AX.X, ALU.add).then_inc(S["route_ready"], 1)
                dve.wait_ge(S["route_ready"], 3 * n + 1)
                V.reciprocal(lrec[:, :], lsum[:, :]).then_inc(S["route_ready"], 1)
                dve.wait_ge(S["route_ready"], 3 * n + 2)
                V.tensor_tensor(route[n % 2][:, :, :], lsel[:, :, :], lrec[:, :].unsqueeze(2).to_broadcast([P, NT, E]),
                                ALU.mult).then_inc(S["route_ready"], 1)

            def attention(n, k):
                g = n % 2
                if k == 0:
                    if n < 2:
                        dve.wait_ge(S[f"ld_x{g}"], 16)
                    else:
                        dve.wait_ge(S["x_ffn"], n - 1)
                    statistics(n, 0)
                if k == 1:
                    normalise(n, 0)
                if k == 2:
                    low_of_xT(n, 0, xa)
                if n < 2:
                    if k == 4:
                        for h in range(2):
                            dve.wait_ge(S["qh_ready"], 2 * n + h + 1)
                            low(qfs[1][:, h, :], qf[n][:, h, :], qfs[0][:, h, :], "ql_ready")
                    if 5 <= k < 5 + NT:
                        t = k - 5
                        i = NT * n + t
                        s = score_b[n][t % 2][:, :].rearrange("p (h k) -> p h k", k=KEYS)
                        dve.wait_ge(S["score_ready"], i + 1)
                        V.tensor_reduce(nmax[:, t, :], s, AX.X, ALU.max, negate=True).then_inc(S["nmax_ready"], 1)
                        dve.wait_ge(S["nmax_ready"], i + 1)
                        V.tensor_tensor(prob[n][:, t, :].rearrange("p (h k) -> p h k", k=KEYS), s,
                                        nmax[:, t, :].unsqueeze(2).to_broadcast([P, HEADS, KEYS]), ALU.add)\
                            .then_inc(S["shifted"], 1)
                    if 10 <= k < 10 + NT:
                        t = k - 10
                        i = NT * n + t
                        dve.wait_ge(S["exp_ready"], i + 1)
                        V.tensor_reduce(psum_[:, t, :], prob[n][:, t, :].rearrange("p (h k) -> p h k", k=KEYS),
                                        AX.X, ALU.add).then_inc(S["sum_ready"], 1)
                        dve.wait_ge(S["sum_ready"], i + 1)
                        V.reciprocal(prec[:, t, :], psum_[:, t, :]).then_inc(S["rec_ready"], 1)
                    if k == 15:
                        residual_attention(n)
                        statistics(n, 1)
                    if k == 16:
                        normalise(n, 1)
                    if k == 17:
                        low_of_xT(n, 1, xf[g])
                    if k == 18:
                        route_tokens(n)
                    if k == 19:
                        route_weights(n)
                else:
                    pr = prob1[:, :, 0:KEYS]
                    if k == 3:
                        s = bs[:, 0:NT * KEYS].rearrange("p (t k) -> p t k", k=KEYS)
                        dve.wait_ge(S["s1_ready"], n - 1)
                        V.tensor_reduce(nmax1[:, :], s, AX.X, ALU.max, negate=True).then_inc(S["s1_nmax"], 1)
                        dve.wait_ge(S["s1_nmax"], n - 1)
                        if n == 3:
                            dve.wait_ge(S["s1_T"], 1)
                        V.tensor_tensor(pr, s, nmax1[:, :].unsqueeze(2).to_broadcast([P, NT, KEYS]), ALU.add)\
                            .then_inc(S["s1_shift"], 1)
                    if k == 4:
                        dve.wait_ge(S["s1_exp"], n - 1)
                        V.tensor_reduce(sum1[:, :], pr, AX.X, ALU.add).then_inc(S["s1_sum"], 1)
                        dve.wait_ge(S["s1_sum"], n - 1)
                        V.reciprocal(rec1[:, :], sum1[:, :]).then_inc(S["s1_rec"], 1)
                        dve.wait_ge(S["s1_rec"], n - 1)
                        V.tensor_tensor(pr, pr, rec1[:, :].unsqueeze(2).to_broadcast([P, NT, KEYS]), ALU.mult)\
                            .then_inc(S["s1_prob"], 1)
                    if k == 6:
                        residual_attention(n)
                        statistics(n, 1)
                    if k == 7:
                        normalise(n, 1)
                    if k == 8:
                        low_of_xT(n, 1, xf[g])
                    if k == 9:
                        route_tokens(n)
                    if k == 10:
                        route_weights(n)

            def gate(n, k, i):
                layer, ff, e, t = n // 2, FF[n // 2], k // 2, 2 * (k % 2) + i
                y = 2 * (MM1_STEPS * n + k) + i
                kept = HID_EXPERTS[layer]
                if t == 0 and n:
                    if e >= kept:
                        dve.wait_ge(S["hidT_ready"], chunks_before(n) + 2 * (e - kept + 1))
                    elif e == 0:
                        dve.wait_ge(S["hidT_ready"], chunks_before(n))
                dve.wait_ge(S["act_ready"], y + 1)
                V.scalar_tensor_tensor(hid[:, t, e % kept * ff:(e % kept + 1) * ff], act_sb[:, y % NA, 0:ff],
                                       route[n % 2][:, t, e:e + 1], yb[y % NY][:, ff:2 * ff],
                                       ALU.mult, ALU.mult).then_inc(S["hid_ready"], 1)

            def experts(n, k):
                layer, g = n // 2, n % 2
                if k == 0:
                    dve.wait_ge(S["route_ready"], 3 * (n + 1))
                if k < MM1_STEPS:
                    gate(n, k, 0)
                if k in TSTEP[layer]:
                    c = chunks_before(n) + TSTEP[layer].index(k)
                    dve.wait_ge(S["hidh_ready"], c + 1)
                    low(hid_t[1][:, c % 2, :], tb[:, :], hid_t[0][:, c % 2, :], "hidl_ready")
                if k < MM1_STEPS:
                    gate(n, k, 1)
                if k == TAIL[layer] + 1:
                    dve.wait_ge(S["oT_ready"], n + 1)
                    xv = x_sb[:, g * NT:(g + 1) * NT, :].rearrange("p t d -> p (t d)")
                    V.scalar_tensor_tensor(xv, ob[:, :], tg[:, 2 + layer:3 + layer], xv, ALU.mult, ALU.add)\
                        .then_inc(S["x_ffn"], 1)

            for expert_steps, attentions, _, parts in SLOTS:
                for n, k in expert_steps:
                    experts(n, k)
                for n, k in attentions:
                    attention(n, k)
                    if (n, k) == (0, 0):
                        key_blocks()
                    if (n, k) == VALUES_AT:
                        prepare_values()
                if 1 in parts:
                    prepare_layer1()

        @block.tensor
        def _(pe):
            T = nc.tensor

            def product3(out, a, b, start=True, stop=True):
                T.matmul(out, a[0], b[0], start=start, stop=False)
                T.matmul(out, a[0], b[1], start=False, stop=False)
                return T.matmul(out, a[1], b[0], start=False, stop=stop)

            pe.wait_ge(S["const_ready"], 1)
            pe.wait_ge(S["ld_ctx"], 16)
            T.transpose(tb[:, 0:NG * KEYS], ctx_sb[:, :], ident[0:NG * KEYS, 0:NG * KEYS]).then_inc(S["ctxT_done"], 1)
            pe.wait_ge(S["const_ready"], 4)
            pe.wait_ge(S["ld_fm"], 32)
            T.matmul(bs[:, 128:384], rep[:, :], fm_t[:, :].unsqueeze(1).to_broadcast([HD, 32, HD]),
                     start=True, stop=True).then_inc(S["wzp_done"], 1)
            pe.wait_ge(S["wz_done"], 1)
            T.matmul(bs[:, 0:1], rep_sgn[:, :], fm_b[:, :], start=True, stop=True).then_inc(S["bz_done"], 1)
            pe.wait_ge(S["ctxT_sb"], 1)
            for g in range(2):
                last = T.matmul(bp[:, g * NG * KEYS:(g + 1) * NG * KEYS], wz[:, g, :], ctx_t[:, :], start=True, stop=True)
            last.then_inc(S["zk_done"], 1)

            def fc_transposes():
                pe.wait_ge(S["fcp_done"], 2)
                for g in range(2):
                    last = T.transpose(tb[:, g * D:(g + 1) * D], fc_p[:, g].rearrange("n s h e -> n (s h e)"), ident[:, :])
                last.then_inc(S["fcT_done"], 1)

            def values_through_fc():
                pe.wait_ge(S["fcl_done"], 1)
                pe.wait_ge(S["kbdl_done"], 4)
                pe.wait_ge(S["kbdh_done"], 4)
                for b in range(NG):
                    for c in range(4):
                        rows = [kb[:, b, c // 2].rearrange("p h k -> p (h k)")[:, (c % 2) * P:(c % 2) * P + P] for kb in kbd]
                        last = product3((ob, tb)[b][:, c * D:(c + 1) * D], rows, [f[:, c // 2, :] for f in fcs])
                    last.then_inc(S["v0_done"], 1)

            def layer1_products(i):
                if i == 0:
                    pe.wait_ge(S["ld_at"], 16 * 6)
                    pe.wait_ge(S["probT_sb"], NT)
                    T.transpose(bp[:, 0:D], wo[:, :], ident[:, :])
                    T.matmul(bp[:, D:2 * D], wk[:, :], wq[:, :], start=True, stop=True)
                    T.matmul(bp[:, 2 * D:2 * D + 1], wk[:, :], bq[:, :], start=True, stop=True).then_inc(S["l1_pe"], 1)
                elif i == 1:
                    pe.wait_ge(S["l1_sb"], 1)
                    pe.wait_ge(S["logit_sb"], 5 + 1)
                    T.matmul(bs[:, 0:D], wv[:, :], wo_t[:, :], start=True, stop=True)
                    T.matmul(bs[0:1, D:2 * D], bv[:, :], wo_t[:, :], start=True, stop=True)
                    T.matmul(bs[:, 256:256 + NG * KEYS], kq[:, :], ctx_t[:, :], start=True, stop=True)
                    T.matmul(bs[0:1, 384:384 + NG * KEYS], bqk[:, :], ctx_t[:, :], start=True, stop=True)\
                        .then_inc(S["l1_pe"], 1)
                else:
                    pe.wait_ge(S["l1_sb"], 2)
                    for b in range(NG):
                        o = bp[0:KEYS, b * D:(b + 1) * D]
                        T.matmul(o, ctx_t[:, b * KEYS:(b + 1) * KEYS], vo[:, :], start=True, stop=False)
                        last = T.matmul(o, ones[:, 0:KEYS], bvo[:, :], start=False, stop=True)
                    last.then_inc(S["l1_pe"], 1)

            def transpose_x(n, which):
                m = order_of_norm(n, which)
                pe.wait_ge(S["xn_ready"], NT * (m + 1))
                if which:
                    pe.wait_ge(S["x_att"], n + 1)
                if n and (n, which) != (1, 0):
                    pe.wait_ge(S["logit_sb"], 5 * (n - 1) + 1)
                if (n, which) == (2, 0):
                    pe.wait_ge(S["l1_sb"], 4)
                for t in range(NT):
                    last = T.transpose((bs if which else main_b[n])[:, t * P:(t + 1) * P], xn[:, t, :], ident[:, :])
                last.then_inc(S["xT_ready"], 1)

            def router(n):
                pe.wait_ge(S["xl_ready"], order_of_norm(n, 1) + 1)
                pe.wait_ge(S["xh_ready"], order_of_norm(n, 1) + 1)
                pe.wait_ge(S["rw_l"], 1)
                for t in range(NT):
                    last = product3(bs[:, t * E:(t + 1) * E], [a[:, t * P:(t + 1) * P] for a in xf[n % 2]],
                                    [r[:, n // 2, :] for r in rws])
                last.then_inc(S["logit_ready"], 1)

            def attention(n, k):
                g = n % 2
                if k == 2:
                    transpose_x(n, 0)
                if n < 2:
                    if k == 3:
                        pe.wait_ge(S["xl_ready"], order_of_norm(n, 0) + 1)
                        pe.wait_ge(S["wzl_done"], 1)
                        pe.wait_ge(S["fk_done"], 1)
                        for h in range(2):
                            product3((main_b[n], prob_b[n])[h][:, :], [w[:, h, :] for w in wzs], [a[:, :] for a in xa])\
                                .then_inc(S["z_ready"], 1)
                    if 5 <= k < 5 + NT:
                        t = k - 5
                        i = NT * n + t
                        if t == 0:
                            pe.wait_ge(S["kbdh_done"], 4)
                            pe.wait_ge(S["kbdl_done"], 4)
                            pe.wait_ge(S["ql_ready"], 2 * n + 2)
                        if t >= 2:
                            pe.wait_ge(S["shifted"], i - 1)
                        for h in range(2):
                            last = product3(score_b[n][t % 2][:, h * 256:(h + 1) * 256],
                                            [q[:, h, t * P:(t + 1) * P] for q in qfs],
                                            [kb[:, g, h].rearrange("p h k -> p (h k)") for kb in kbd])
                        last.then_inc(S["score_ready"], 1)
                    if 12 <= k < 12 + NT:
                        t = k - 12
                        pe.wait_ge(S["probT_sb"], NT * n + t + 1)
                        pe.wait_ge(S["v0_sb"], 2)
                        pe.wait_ge(S["shifted"], NT * (n + 1))
                        o = main_b[n][:, t * D:(t + 1) * D]
                        T.matmul(o, ones[:, :], fcb[:, :], start=True, stop=False)
                        for c in range(4):
                            last = T.matmul(o, prob_t[:, t % 2, c, :], v0[:, g, c, :], start=False, stop=(c == 3))
                        if t == NT - 1:
                            last.then_inc(S["att_ready"], 1)
                    if 11 <= k < 11 + NT:
                        t = k - 11
                        pe.wait_ge(S["prob_ready"], NT * n + t + 1)
                        if t:
                            pe.wait_ge(S["probT_sb"], NT * n + t)
                        for c in range(4):
                            last = T.transpose(prob_b[n][:, c * P:(c + 1) * P], prob[n][:, t, c * P:(c + 1) * P], ident[:, :])
                        last.then_inc(S["probT_ready"], 1)
                    if k == 17:
                        transpose_x(n, 1)
                    if k == 18:
                        router(n)
                else:
                    if k == 3:
                        pe.wait_ge(S["xl_ready"], order_of_norm(n, 0) + 1)
                        pe.wait_ge(S["l1_sb"], 4)
                        for t in range(NT):
                            o = bs[:, t * KEYS:(t + 1) * KEYS]
                            product3(o, [a[:, t * P:(t + 1) * P] for a in xa],
                                     [m[:, g * KEYS:(g + 1) * KEYS] for m in m1s], stop=False)
                            last = T.matmul(o, ones[:, :], c1[:, g * KEYS:(g + 1) * KEYS], start=False, stop=True)
                        last.then_inc(S["s1_ready"], 1)
                    if k == 5:
                        pe.wait_ge(S["s1_prob"], n - 1)
                        pe.wait_ge(S["one_col"], 1)
                        for t in range(NT):
                            last = T.transpose(bp[0:KEYS + 1, t * P:(t + 1) * P], prob1[:, t, :], ident[:, :])
                        last.then_inc(S["s1_T"], 1)
                    if k == 6:
                        pe.wait_ge(S["s1_T_sb"], n - 1)
                        pe.wait_ge(S["ld_bo"], 32)
                        for t in range(NT):
                            last = T.matmul(bs[:, t * D:(t + 1) * D], prob1_t[:, t, :], v1[:, g, :], start=True, stop=True)
                        last.then_inc(S["att_ready"], 1)
                    if k == 8:
                        transpose_x(n, 1)
                    if k == 9:
                        router(n)

            def first_product(n, k, i):
                layer, t = n // 2, 2 * (k % 2) + i
                y = 2 * (MM1_STEPS * n + k) + i
                if y >= NY:
                    pe.wait_ge(S["hid_ready"], y - NY + 1)
                elif y == 0:
                    pe.wait_ge(S["x_att"], 2)
                product3(yb[y % NY][:, 0:2 * FF[layer]], [a[:, t * P:(t + 1) * P] for a in xf[n % 2]],
                         [v[:, k // 2, :, :].rearrange("p s f -> p (s f)") for v in (wa_h[layer], wa_l[layer])])\
                    .then_inc(S["y_ready"], 1)

            def experts(n, k):
                layer, ff = n // 2, FF[n // 2]
                if k < MM1_STEPS:
                    if k == 0:
                        pe.wait_ge(S["xh_ready"], order_of_norm(n, 1) + 1)
                        pe.wait_ge(S["xl_ready"], order_of_norm(n, 1) + 1)
                    pe.wait_ge(S["wsplit_h"], wa_pieces(layer, k // 2))
                    pe.wait_ge(S["wsplit_l"], wa_pieces(layer, k // 2))
                    first_product(n, k, 0)
                if k in TSTEP[layer]:
                    i = TSTEP[layer].index(k)
                    c = chunks_before(n) + i
                    last_expert = (i * P + P - 1) // ff
                    pe.wait_ge(S["hid_ready"], 2 * MM1_STEPS * n + NT * (last_expert + 1))
                    if c:
                        pe.wait_ge(S["hidl_ready"], c)
                    col = i * P % (HID_EXPERTS[layer] * ff)
                    for t in range(NT):
                        last = T.transpose(tb[:, t * P:(t + 1) * P], hid[:, t, col:col + P], ident[:, :])
                    last.then_inc(S["hidT_ready"], 1)
                if k < MM1_STEPS:
                    first_product(n, k, 1)
                if k - 1 in TSTEP[layer]:
                    i = TSTEP[layer].index(k - 1)
                    c = chunks_before(n) + i
                    pe.wait_ge(S["hidh_ready"], c + 1)
                    pe.wait_ge(S["hidl_ready"], c + 1)
                    pe.wait_ge(S["wsplit_l"], wb_pieces(layer, i))
                    if i == 0 and n:
                        pe.wait_ge(S["x_ffn"], n)
                    product3(ob[:, :], [w[:, i, :] for w in (wb_h[layer], wb_l[layer])],
                             [h[:, c % 2, :] for h in hid_t], start=(i == 0), stop=(i == NCH[layer] - 1))\
                        .then_inc(S["mm2_done"], 1)
                if k == TAIL[layer] + 1:
                    pe.wait_ge(S["o_sb"], n + 1)
                    for t in range(NT):
                        last = T.transpose(ob[:, t * P:(t + 1) * P], o_t[:, t * P:(t + 1) * P], ident[:, :])
                    last.then_inc(S["oT_ready"], 1)

            for expert_steps, attentions, _, parts in SLOTS:
                for n, k in expert_steps:
                    experts(n, k)
                for n, k in attentions:
                    attention(n, k)
                    if (n, k) == VALUES_AT:
                        fc_transposes()
                        values_through_fc()
                for i in parts:
                    layer1_products(i)


_INS = ['x', 'ctx_1024', 'g_xattn', 'g_ffn', 'L0_xattn_fm_w', 'L0_xattn_fm_b', 'L0_xattn_fc_w', 'L0_xattn_fc_b',
        'L0_ffn_router_weight', 'L0_ffn_w1', 'L0_ffn_w2', 'L1_xattn_Wk', 'L1_xattn_Wv', 'L1_xattn_bv',
        'L1_xattn_Wq', 'L1_xattn_bq', 'L1_xattn_Wo', 'L1_xattn_bo', 'L1_ffn_w_gate', 'L1_ffn_w1', 'L1_ffn_w3',
        'L1_ffn_w2']


def kernel(**inputs):
    import numpy as _np
    import concourse.bacc as _bacc
    from concourse import mybir as _mybir
    from concourse.bass_utils import run_bass_kernel_spmd as _run

    nc = _bacc.Bacc("TRN2", target_bir_lowering=False, num_devices=1)
    arrays, args = {}, []
    for name in _INS:
        a = _np.ascontiguousarray(inputs[name])
        arrays[f"in_{name}_dram"] = a
        args.append(nc.dram_tensor(f"in_{name}_dram", a.shape, _mybir.dt.from_np(a.dtype), kind="ExternalInput").ap())
    args.append(nc.dram_tensor("out_0_dram", (2, 512, 128), _mybir.dt.float32, kind="ExternalOutput").ap())
    build(nc, *args)
    r = _run(nc, [arrays], core_ids=[0])
    return r.results[0]["out_0_dram"]
```

```python
import concourse.bass as bass
from concourse import mybir
from contextlib import ExitStack

P = 128
D = 128
TOK = 512
NT = TOK // P
NG = 2
KEYS = 32
HEADS, HD = 16, 8
HG = 8
E = 8
FF = (176, 256)
NCH = tuple(E * f // P for f in FF)
EPS = 1e-5
SCALE = 1.0 / float(D) ** 0.5
NY = 4
NA = 4
HID_EXPERTS = (8, 5)

MM1_STEPS = NT * E
T_DELAY = (5, 5)
M_DELAY = 3


def chunk_steps(n):
    steps = []
    for c in range(NCH[n // 2]):
        last_expert = (c * P + P - 1) // FF[n // 2]
        steps.append(max(NT * last_expert + T_DELAY[n // 2], steps[-1] + 2 if steps else 0))
    if n == 3:
        steps[-1] -= 1
    return steps


TSTEP = [chunk_steps(n) for n in range(4)]
TAIL = [s[-1] + M_DELAY + 1 for s in TSTEP]
F_STEPS = [t + 3 for t in TAIL]

K_SUM = 7
K_T = K_SUM + 2
K_PV = K_T + 1
K_RES = K_PV + NT - 1
K_ROUTER = K_RES + 3
A_STEPS = (K_ROUTER + 2, 11)
VALUES_STEP = 7
KEY_BLOCKS_STEP = 1
WPIECES = 18


def chunks_before(n):
    return sum(NCH[m // 2] for m in range(n))


def hid_slot(n, e):
    return e if n < 2 else (e + E * (n - 2)) % HID_EXPERTS[1]


def order_of_norm(n, which):
    return 2 * which + n if n < 2 else 2 * n + which


A_LAG = 3
AFTER_RES = ((1, 3, 4, 5), (4, 7, 9, 10))
AFTER_FFN = {2: (0, 2, 4, 6, 8, 11, 12, 15, 17, 19, 21),
             3: (0, 2, 4, 6, 8, 12, 14, 16, 18, 20, 22)}
SPLITS_0 = (6, 8, 10, 12, 16, 18)
SPLITS_1 = tuple(range(1, 2 * (WPIECES - 6), 2))
PARTS_AT = (11, 15, 19)
CLOCK_PRODUCTS = (9, 4, 4)


def slots():
    at0, at1 = ([2 * (A_LAG * n + k) for k in range(K_RES + 1)]
                + [2 * (A_LAG * n + K_RES) + s for s in AFTER_RES[n]] for n in range(2))
    first = max(at1[K_RES], at0[-1]) + 1
    f_start = [first + n * MM1_STEPS for n in range(4)]
    table = [([], [], [], []) for _ in range(f_start[3] + F_STEPS[3])]
    for n in range(4):
        for k in range(F_STEPS[n]):
            table[f_start[n] + k][0].append((n, k))
    for n in range(2):
        for k, at in enumerate((at0, at1)[n]):
            table[at][1].append((n, k))
    for n, offsets in AFTER_FFN.items():
        start = f_start[n - 2] + TAIL[n - 2] + 2
        assert start + offsets[-1] < f_start[n]
        for k, at in enumerate(offsets):
            table[start + at][1].append((n, k))
    for i, at in enumerate(SPLITS_0 + tuple(first + at for at in SPLITS_1)):
        table[at][2].append(i)
    for i, at in enumerate(PARTS_AT):
        table[first + at][3].append(i)
    return table


SLOTS = slots()


def build(nc, x_d, ctx_d, gx_d, gf_d, fmw_d, fmb_d, fcw_d, fcb_d, rw0_d, w1_d, w2_d,
          wk_d, wv_d, bv_d, wq_d, bq_d, wo_d, bo_d, rw1_d, u1_d, u3_d, u2_d, out_d):
    f32, f32r = mybir.dt.float32, mybir.dt.float32r
    ALU, ACT, AX = mybir.AluOpType, mybir.ActivationFunctionType, mybir.AxisListType
    stack = ExitStack()
    with stack:
        def sb(name, shape, dt=f32):
            return stack.enter_context(nc.sbuf_tensor(name, shape, dt))

        def sem(name):
            return stack.enter_context(nc.semaphore(name))

        x_sb = sb("x_sb", [P, NG * NT, D])
        stats = sb("stats", [P, NT, 6])
        mv = sb("mv", [P, NT, 2])
        rstd = sb("rstd", [P, NT])
        varp = sb("varp", [P, NT])
        half = sb("half", [P, NT])
        xn = sb("xn", [P, NT, D])
        xt = [sb(f"xt{g}", [P, TOK]) for g in range(NG)]
        xf = [[sb(f"xf{g}{i}", [P, TOK], f32r) for i in "hl"] for g in range(NG)]

        ident = sb("ident", [P, P])
        ones = sb("ones", [1, P])
        sgn_mask = sb("sgn_mask", [P, 2, 2, HG * HD])
        key_mask = sb("key_mask", [P, HG, KEYS])
        rep = sb("rep", [HD, P])
        rep_sgn = sb("rep_sgn", [HD, P])
        fm_t = sb("fm_t", [HD, HD])
        fm_b = sb("fm_b", [HD, 1])
        wz = sb("wz", [P, 2, P])
        bz = sb("bz", [P, 1])
        ctx_sb = sb("ctx_sb", [NG * KEYS, D])
        ctx_t = sb("ctx_t", [D, NG * KEYS])
        fk = sb("fk", [P, 2, NG * KEYS])
        kbd = sb("kbd", [P, NG, 2, HG, KEYS])
        fc_t = sb("fc_t", [P, 2, D])
        fcb = sb("fcb", [P, D])
        v0 = sb("v0", [P, NG, 4, D])
        gates = sb("gates", [P, 4])
        tg = sb("tg", [P, 4])

        wq, wk, wv, wo = (sb(n, [D, D]) for n in ("wq", "wk", "wv", "wo"))
        bq, bv = sb("bq", [D, 1]), sb("bv", [D, 1])
        wo_t = sb("wo_t", [D, D])
        kq = sb("kq", [D, D])
        vo = sb("vo", [D, D])
        bqk = sb("bqk", [D, 1])
        bvo = sb("bvo", [1, D])
        m1 = sb("m1", [D, NG * KEYS])
        c1 = sb("c1", [P, NG * KEYS])
        v1 = sb("v1", [KEYS + 1, NG, D])

        nmax = sb("nmax", [P, NT, HEADS])
        hid = sb("hid", [P, NT, NCH[0] * P])
        prob = [sb("prob", [P, NT, HEADS * KEYS])[:, :, :], hid[:, :, 0:HEADS * KEYS]]
        qf = [sb("qf", [P, 2, TOK])[:, :, :], hid[:, 1:3, 512:1024]]
        fc_sb = hid[:, 0, 512:768].rearrange("n (g h s e) -> n g h s e", g=2, h=HG, s=2)
        fc_p = hid[:, 0, 768:1024].rearrange("n (g s h e) -> n g s h e", g=2, s=2, h=HG)
        psum_ = sb("psum_", [P, NT, HEADS])
        prec = sb("prec", [P, NT, HEADS])
        prob_t = sb("prob_t", [P, 2, 4, P])
        prob1 = sb("prob1", [P, NT, KEYS + 1])
        nmax1, sum1, rec1 = sb("nmax1", [P, NT]), sb("sum1", [P, NT]), sb("rec1", [P, NT])
        prob1_t = sb("prob1_t", [KEYS + 1, NT, P])

        rw = sb("rw", [D, 2, E])
        logit = sb("logit", [P, NT, E])
        before = sb("before", [P, E, E])
        cmp_gt = xn[:, 0:2, :].rearrange("p a (b i j) -> p (a b) i j", i=E, j=E)
        cmp_eq = xn[:, 2:4, :].rearrange("p a (b i j) -> p (a b) i j", i=E, j=E)
        rank = sb("rank", [P, NT, E])
        lmax = sb("lmax", [P, NT])
        ldiff = sb("ldiff", [P, NT, E])
        lexp = sb("lexp", [P, NT, E])
        lsel = sb("lsel", [P, NT, E])
        lsum, lrec = sb("lsum", [P, NT]), sb("lrec", [P, NT])
        route = [sb(f"route{g}", [P, NT, E]) for g in range(NG)]

        stage = sb("stage", [P, 2 * E * FF[0] + NCH[0] * P])
        wa_f = [stage[:, 0:2 * E * ff].rearrange("p (e s f) -> p e s f", e=E, s=2) for ff in FF]
        wb_f = [stage[:, 2 * E * FF[0]:].rearrange("p (c n) -> p c n", n=D),
                stage[:, 0:NCH[1] * D].rearrange("p (c n) -> p c n", n=D)]
        wa_l = [sb(f"wal{l}", [D, E, 2, FF[l]], f32r) for l in range(2)]
        wa_h = [sb(f"wah{l}", [D, E, 2, FF[l]], f32r) for l in range(2)]
        wb_h = [sb(f"wbh{l}", [P, NCH[l], D], f32r) for l in range(2)]
        wb_l = [sb(f"wbl{l}", [P, NCH[l], D], f32r) for l in range(2)]
        act_sb = sb("act_sb", [P, NA, FF[1]])
        hid_t = [sb(f"hid_t{i}", [P, 2, TOK], f32r) for i in "hl"]
        o_t = sb("o_t", [D, TOK])

        bank = [stack.enter_context(nc.psum_tensor(f"bank{i}", [P, 512], f32)) for i in range(8)]
        yb, tb, ob = bank[0:NY], bank[4], bank[5]
        bs, bp = bank[6], bank[7]

        names = """ld_x0 ld_x1 ld_ctx ld_fm ld_fc ld_fb ld_g ld_r ld_at ld_bo ld_w0 ld_w1 ld_w2 ld_w3 ld_w4 ld_w5 ld_w6 ld_w7 ld_w8 ld_w9 out_done
            const_ready pool_own rstd_ready
            wzp_done wz_done bz_done ctxT_done ctxT_sb zk_done fk_done
            kbd_done fcp_done fcT_done fcT_sb v0_done v0_sb tg_done bias_ready x_bias
            l1_pe l1_sb one_col
            stats_ready mv_ready xn_ready xT_ready xt_sb xh_ready xl_ready
            z_ready qf_ready score_ready nmax_ready shifted exp_ready sum_ready rec_ready
            prob_ready probT_ready probT_sb att_ready x_att
            s1_ready s1_bias s1_nmax s1_shift s1_exp s1_sum s1_rec s1_prob s1_T s1_T_sb
            logit_ready logit_sb router_dve lexp_ready route_ready
            wsplit_h wsplit_l
            y_ready act_ready hid_ready hidT_ready hidh_ready hidl_ready mm2_done o_sb oT_ready x_ffn"""
        S = {n: sem(n) for n in names.split()}

        block = stack.enter_context(nc.Block())

        score_b = [(bs, yb[2]), (yb[0], yb[3])]
        main_b = [bs, yb[0], bs, bs]
        prob_b = [bp, yb[1], bp, bp]
        att_b = [ob, tb, bs, bs]

        def tbank(n, i):
            return bs if n == 3 and i % 2 else tb


        def flat(t):
            return t.rearrange("p e s f -> p e (s f)")

        pieces = []
        for q in range(4):
            pieces.append([v[:, 2 * q:2 * q + 2, :] for v in (flat(wa_f[0]), flat(wa_h[0][:, :, :, :]), flat(wa_l[0][:, :, :, :]))])
        for a, b in ((0, 6), (6, NCH[0])):
            pieces.append([v[:, a:b, :] for v in (wb_f[0], wb_h[0], wb_l[0])])
        for q in range(8):
            pieces.append([v[:, q:q + 1, :] for v in (flat(wa_f[1]), flat(wa_h[1][:, :, :, :]), flat(wa_l[1][:, :, :, :]))])
        for q in range(4):
            pieces.append([v[:, 4 * q:4 * q + 4, :] for v in (wb_f[1], wb_h[1], wb_l[1])])
        assert len(pieces) == WPIECES
        load_of = [0, 1, 2, 3, 4, 4] + [5, 5, 6, 6, 7, 7, 8, 8] + [9] * 4
        landed = [32 if 5 <= i <= 8 else 16 for i in load_of]
        def wa_pieces(layer, e):
            return e // 2 + 1 if layer == 0 else 6 + e + 1

        def wb_pieces(layer, c):
            return (5 if c < 6 else 6) if layer == 0 else 14 + c // 4 + 1

        @block.sync
        def _(sp):
            def load(dst, src, s):
                sp.dma_start(dst, src).then_inc(S[s], 16)
            load(x_sb[:, 0:NT, :], x_d[0].rearrange("(t p) d -> p t d", p=P), "ld_x0")
            load(ctx_sb[:, :], ctx_d.rearrange("b k d -> (b k) d"), "ld_ctx")
            load(x_sb[:, NT:2 * NT, :], x_d[1].rearrange("(t p) d -> p t d", p=P), "ld_x1")
            load(fc_sb[:, :, :, :, :], fcw_d.rearrange("n (g h s e) -> n g h s e", g=2, h=HG, s=2), "ld_fc")
            load(fcb[:, :], fcb_d.rearrange("(a n) -> a n", a=1).to_broadcast([P, D]), "ld_fb")
            for q in range(4):
                load(wa_f[0][:, 2 * q:2 * q + 2, :, :].rearrange("p e s f -> p e (s f)"),
                     w1_d[2 * q:2 * q + 2].rearrange("e p f -> p e f"), f"ld_w{q}")
            load(wb_f[0][:, :, :], w2_d.rearrange("e f n -> (e f) n").rearrange("(c p) n -> p c n", p=P), "ld_w4")
            for i, r in enumerate((rw0_d, rw1_d)):
                load(rw[:, i, :], r, "ld_r")
            for dst, src in ((wq, wq_d), (wk, wk_d), (wv, wv_d), (wo, wo_d)):
                load(dst[:, :], src, "ld_at")
            for dst, src in ((bq, bq_d), (bv, bv_d)):
                load(dst[:, :], src.rearrange("(d a) -> d a", a=1), "ld_at")
            for b in range(NG):
                load(v1[KEYS:KEYS + 1, b, :], bo_d.rearrange("(a n) -> a n", a=1), "ld_bo")
            for q in range(4):
                if q == 0:
                    sp.wait_ge(S["wsplit_l"], 4)
                if q == 2:
                    sp.wait_ge(S["wsplit_l"], 6)
                for s, w in enumerate((u1_d, u3_d)):
                    load(wa_f[1][:, 2 * q:2 * q + 2, s, :], w[2 * q:2 * q + 2].rearrange("e p f -> p e f"), f"ld_w{5 + q}")
            sp.wait_ge(S["wsplit_l"], 10)
            load(wb_f[1][:, :, :], u2_d.rearrange("e f n -> (e f) n").rearrange("(c p) n -> p c n", p=P), "ld_w9")
            for g in range(NG):
                sp.wait_ge(S["x_ffn"], NG + g + 1)
                sp.dma_start(out_d[g].rearrange("(t p) d -> p t d", p=P),
                             x_sb[:, g * NT:(g + 1) * NT, :]).then_inc(S["out_done"], 16)
            sp.wait_ge(S["out_done"], 16 * NG)

        @block.gpsimd
        def _(pool):
            own = [0]

            def step(ins):
                own[0] += 1
                ins.then_inc(S["pool_own"], 1)
                pool.wait_ge(S["pool_own"], own[0])

            def select(ap, pattern, base, cm, op, fill):
                return pool.affine_select(out=ap, in_=ap, compare_op=op, fill=fill, base=base,
                                          pattern=pattern, channel_multiplier=cm)

            step(pool.memset(ident[:, :], 0.0))
            select(ident[:, :], [[-1, P]], 0, 1, ALU.not_equal, 1.0).then_inc(S["const_ready"], 1)
            pool.memset(rep[:, :], 0.0)
            step(pool.memset(rep_sgn[:, :], 0.0))
            select(rep[:, :].rearrange("p (h d) -> p h d", d=HD), [[0, HEADS], [-1, HD]], 0, 1,
                   ALU.not_equal, 1.0).then_inc(S["const_ready"], 1)
            for s, sign in enumerate((1.0, -1.0)):
                select(rep_sgn[:, s * 64:s * 64 + 64].rearrange("p (h d) -> p h d", d=HD), [[0, HG], [-1, HD]], 0, 1,
                       ALU.not_equal, sign).then_inc(S["const_ready"], 1)
            pool.memset(sgn_mask[:, :, 0, :], 1.0)
            step(pool.memset(sgn_mask[:, :, 1, :], -1.0))
            for g in range(2):
                v = sgn_mask[:, g, :, :].rearrange("p s (h e) -> p s h e", e=HD)
                step(select(v, [[0, 2], [-HD, HG], [0, HD]], -64 * g, 1, ALU.is_ge, 0.0))
                select(v, [[0, 2], [HD, HG], [0, HD]], 64 * g + HD - 1, -1, ALU.is_ge, 0.0)\
                    .then_inc(S["const_ready"], 1)
            pool.memset(half[:, :], -0.5)
            pool.memset(ones[:, :], 1.0).then_inc(S["const_ready"], 1)

            def late_constants():
                step(pool.memset(key_mask[:, :, :], 1.0))
                for r in range(2):
                    v = key_mask[64 * r:64 * r + 64, :, :]
                    step(select(v, [[-HD, HG], [0, KEYS]], 0, 1, ALU.is_ge, 0.0))
                    select(v, [[HD, HG], [0, KEYS]], HD - 1, -1, ALU.is_ge, 0.0).then_inc(S["const_ready"], 1)
                    pool.wait_ge(S["const_ready"], 8 + r)
                step(pool.memset(before[:, :, :], 1.0))
                select(before[:, :, :], [[1, E], [-1, E]], 0, 0, ALU.is_gt, 0.0).then_inc(S["const_ready"], 1)
                pool.memset(prob1[:, :, KEYS:KEYS + 1], 1.0).then_inc(S["one_col"], 1)

            def rstd_of(n, which):
                m = order_of_norm(n, which)
                pool.wait_ge(S["mv_ready"], NT * (m + 1))
                step(pool.tensor_scalar(varp[:, :], mv[:, :, 1], EPS, None, ALU.add))
                pool.tensor_tensor(rstd[:, :], varp[:, :], half[:, :], ALU.pow).then_inc(S["rstd_ready"], 1)

            def attention(n, k):
                if k == 0:
                    rstd_of(n, 0)
                if (n, k) == (0, 0):
                    late_constants()
                    pool.wait_ge(S["ld_fc"], 16)
                    for g in range(2):
                        pool.tensor_copy(fc_p[:, g], fc_sb[:, g].rearrange("n h s e -> n s h e"))\
                            .then_inc(S["fcp_done"], 1)
                if n < 2:
                    if k == 3:
                        if n == 0:
                            pool.wait_ge(S["ld_fb"], 16)
                            pool.wait_ge(S["tg_done"], 1)
                            pool.tensor_scalar(fcb[:, :], fcb[:, :], tg[:, 0:1], None, ALU.mult).then_inc(S["bias_ready"], 1)
                            pool.wait_ge(S["bias_ready"], 1)
                        pool.wait_ge(S["xn_ready"], NT * (n + 1))
                        xv = x_sb[:, n * NT:(n + 1) * NT, :]
                        pool.tensor_tensor(xv, xv, fcb[:, :].unsqueeze(1).to_broadcast([P, NT, D]), ALU.add)\
                            .then_inc(S["x_bias"], 1)
                    if K_SUM <= k < K_SUM + NT:
                        t = k - K_SUM
                        pool.wait_ge(S["rec_ready"], NT * n + t + 1)
                        v = prob[n][:, t, :].rearrange("p (h k) -> p h k", k=KEYS)
                        pool.tensor_tensor(v, v, prec[:, t, :].unsqueeze(2).to_broadcast([P, HEADS, KEYS]),
                                           ALU.mult).then_inc(S["prob_ready"], 1)
                    if k == K_RES:
                        rstd_of(n, 1)
                elif k == 6:
                    rstd_of(n, 1)

            def split(i):
                full, h, l = pieces[i]
                pool.wait_ge(S["wsplit_h"], i + 1)
                pool.tensor_tensor(l, full, h.bitcast(f32), ALU.subtract).then_inc(S["wsplit_l"], 1)

            for _, attentions, split_pieces, _ in SLOTS:
                for n, k in attentions:
                    attention(n, k)
                for i in split_pieces:
                    split(i)

        @block.scalar
        def _(act):
            act.dma_start(fm_t[:, :], fmw_d.rearrange("e d -> d e"), allow_slow_non_contiguous=True)\
                .then_inc(S["ld_fm"], 16)
            act.dma_start(fm_b[:, :], fmb_d.rearrange("(d a) -> d a", a=1)).then_inc(S["ld_fm"], 16)
            for i, g in enumerate((gx_d, gf_d)):
                act.dma_start(gates[:, 2 * i:2 * i + 2], g.rearrange("(a n) -> a n", a=1).to_broadcast([P, 2]))\
                    .then_inc(S["ld_g"], 16)
            def copy(dst, src):
                return nc.scalar.activation(dst, src, ACT.Copy)

            act.wait_ge(S["ctxT_done"], 1)
            copy(ctx_t[:, :], tb[:, 0:NG * KEYS]).then_inc(S["ctxT_sb"], 1)
            act.wait_ge(S["bz_done"], 1)
            copy(bz[:, :], bs[:, 0:1]).then_inc(S["bz_done"], 1)
            act.wait_ge(S["zk_done"], 1)
            act.wait_ge(S["bz_done"], 2)
            nc.scalar.activation(fk[:, :, :].rearrange("p g k -> p (g k)"), bp[:, 0:2 * NG * KEYS], ACT.Exp,
                                 bias=bz[:, 0:1]).then_inc(S["fk_done"], 1)
            act.wait_ge(S["ld_g"], 32)
            nc.scalar.activation(tg[:, :], gates[:, :], ACT.Tanh).then_inc(S["tg_done"], 1)

            def prepare_values():
                act.wait_ge(S["fcT_done"], 1)
                copy(fc_t[:, :, :].rearrange("p g n -> p (g n)"), tb[:, 0:2 * D]).then_inc(S["fcT_sb"], 1)
                for b in range(NG):
                    act.wait_ge(S["v0_done"], b + 1)
                    copy(v0[:, b, :, :].rearrange("p c n -> p (c n)"), (ob, tb)[b][:, :]).then_inc(S["v0_sb"], 1)

            def prepare_layer1(i):
                act.wait_ge(S["l1_pe"], i + 1)
                if i == 0:
                    copy(wo_t[:, :], bp[:, 0:D])
                    copy(kq[:, :], bp[:, D:2 * D])
                    copy(bqk[:, :], bp[:, 2 * D:2 * D + 1]).then_inc(S["l1_sb"], 1)
                elif i == 1:
                    copy(vo[:, :], bs[:, 0:D])
                    copy(bvo[:, :], bs[0:1, D:2 * D])
                    copy(m1[:, :], bs[:, 256:256 + NG * KEYS])
                    copy(c1[:, :], bs[:, 384:384 + NG * KEYS]).then_inc(S["l1_sb"], 1)
                else:
                    copy(v1[0:KEYS, :, :].rearrange("k b n -> k (b n)"), bp[0:KEYS, 0:NG * D]).then_inc(S["l1_sb"], 1)

            def copy_xT(n, which):
                act.wait_ge(S["xT_ready"], order_of_norm(n, which) + 1)
                copy(xt[n % 2][:, :], (bs if which else main_b[n])[:, :]).then_inc(S["xt_sb"], 1)
                if which:
                    copy(xf[n % 2][0][:, :], bs[:, :]).then_inc(S["xh_ready"], 1)

            def router_exp(n):
                act.wait_ge(S["router_dve"], 3 * n + 2)
                nc.scalar.activation(lexp[:, :, :], ldiff[:, :, :], ACT.Exp).then_inc(S["lexp_ready"], 1)

            def attention(n, k):
                g = n % 2
                if k == 2:
                    copy_xT(n, 0)
                if n < 2:
                    if k == 3:
                        for h in range(2):
                            act.wait_ge(S["z_ready"], 2 * n + h + 1)
                            nc.scalar.activation(qf[n][:, h, :], (main_b[n], prob_b[n])[h][:, :], ACT.Exp,
                                                 bias=bz[:, 0:1]).then_inc(S["qf_ready"], 1)
                    if 6 <= k < 6 + NT:
                        t = k - 6
                        act.wait_ge(S["shifted"], NT * n + t + 1)
                        nc.scalar.activation(prob[n][:, t, :], prob[n][:, t, :], ACT.Exp,
                                             scale=SCALE).then_inc(S["exp_ready"], 1)
                    if K_T <= k < K_T + NT:
                        t = k - K_T
                        act.wait_ge(S["probT_ready"], NT * n + t + 1)
                        copy(prob_t[:, t % 2].rearrange("p c q -> p (c q)"), prob_b[n][:, :]).then_inc(S["probT_sb"], 1)
                    if k == K_RES + 2:
                        copy_xT(n, 1)
                    if k == K_ROUTER:
                        router_exp(n)
                else:
                    if k == 3:
                        act.wait_ge(S["s1_shift"], n - 1)
                        nc.scalar.activation(prob1[:, :, 0:KEYS], prob1[:, :, 0:KEYS], ACT.Exp,
                                             scale=SCALE).then_inc(S["s1_exp"], 1)
                    if k == 5:
                        act.wait_ge(S["s1_T"], n - 1)
                        copy(prob1_t[:, :, :].rearrange("k t q -> k (t q)"), bp[0:KEYS + 1, :]).then_inc(S["s1_T_sb"], 1)
                    if k == 8:
                        copy_xT(n, 1)
                    if k == 9:
                        router_exp(n)

            def silu(n, k):
                y = MM1_STEPS * n + k
                ff = FF[n // 2]
                act.wait_ge(S["y_ready"], y + 1)
                if y >= NA:
                    act.wait_ge(S["hid_ready"], y - NA + 1)
                nc.scalar.activation(act_sb[:, y % NA, 0:ff], yb[y % NY][:, 0:ff], ACT.Silu)\
                    .then_inc(S["act_ready"], 1)

            def experts(n, k):
                layer = n // 2
                if k < MM1_STEPS:
                    silu(n, k)
                if k in TSTEP[n]:
                    c = chunks_before(n) + TSTEP[n].index(k)
                    act.wait_ge(S["hidT_ready"], c + 1)
                    if c >= 2:
                        act.wait_ge(S["mm2_done"], c - 1)
                    copy(hid_t[0][:, c % 2, :], tbank(n, c - chunks_before(n))[:, :]).then_inc(S["hidh_ready"], 1)
                if k == TAIL[n]:
                    act.wait_ge(S["mm2_done"], chunks_before(n + 1))
                    copy(o_t[:, :], ob[:, :]).then_inc(S["o_sb"], 1)

            def split(i):
                full, h, l = pieces[i]
                act.wait_ge(S[f"ld_w{load_of[i]}"], landed[i])
                if i == 6:
                    act.wait_ge(S["x_att"], 2)
                copy(h, full).then_inc(S["wsplit_h"], 1)

            for expert_steps, attentions, split_pieces, parts in SLOTS:
                for n, k in expert_steps:
                    experts(n, k)
                for n, k in attentions:
                    attention(n, k)
                    if (n, k) == (0, VALUES_STEP):
                        prepare_values()
                for i in split_pieces:
                    split(i)
                for i in parts:
                    prepare_layer1(i)

        @block.vector
        def _(dve):
            V = nc.vector

            def low(dst, full, high, s):
                V.tensor_tensor(dst, full, high.bitcast(f32), ALU.subtract).then_inc(S[s], 1)

            def feature_weights():
                dve.wait_ge(S["wzp_done"], 1)
                dve.wait_ge(S["const_ready"], 6)
                V.tensor_tensor(wz[:, :, :].rearrange("p g c -> p (g c)"), bs[:, 128:384],
                                sgn_mask[:, :, :, :].rearrange("p g s c -> p (g s c)"), ALU.mult).then_inc(S["wz_done"], 1)

            def key_blocks():
                dve.wait_ge(S["fk_done"], 1)
                dve.wait_ge(S["const_ready"], 9)
                for b in range(NG):
                    for g in range(2):
                        V.tensor_tensor(kbd[:, b, g], key_mask[:, :, :],
                                        fk[:, g, b * KEYS:(b + 1) * KEYS].unsqueeze(1)
                                        .to_broadcast([P, HG, KEYS]), ALU.mult).then_inc(S["kbd_done"], 1)

            def statistics(n, which):
                m, g = order_of_norm(n, which), n % 2
                for t in range(NT):
                    V.bn_stats(stats[:, t, :], x_sb[:, g * NT + t, :]).then_inc(S["stats_ready"], 1)
                for t in range(NT):
                    dve.wait_ge(S["stats_ready"], NT * m + t + 1)
                    V.bn_aggr(mv[:, t, :], stats[:, t, :]).then_inc(S["mv_ready"], 1)

            def normalise(n, which):
                m, g = order_of_norm(n, which), n % 2
                dve.wait_ge(S["rstd_ready"], m + 1)
                if m:
                    dve.wait_ge(S["xT_ready"], m)
                for t in range(NT):
                    V.tensor_scalar(xn[:, t, :], x_sb[:, g * NT + t, :], mv[:, t, 0:1], rstd[:, t:t + 1],
                                    ALU.subtract, ALU.mult).then_inc(S["xn_ready"], 1)

            def low_of_xT(n):
                dve.wait_ge(S["xh_ready"], n + 1)
                low(xf[n % 2][1][:, :], bs[:, :], xf[n % 2][0][:, :], "xl_ready")

            def residual_attention(n):
                g = n % 2
                dve.wait_ge(S["att_ready"], n + 1)
                dve.wait_ge(S["tg_done"], 1)
                dve.wait_ge(S["x_bias"], min(n + 1, 2))
                xv = x_sb[:, g * NT:(g + 1) * NT, :].rearrange("p t d -> p (t d)")
                V.scalar_tensor_tensor(xv, att_b[n][:, :], tg[:, n // 2:n // 2 + 1], xv, ALU.mult, ALU.add)\
                    .then_inc(S["x_att"], 1)
                dve.wait_ge(S["x_att"], n + 1)

            def route_tokens(n):
                own = 3 * n
                dve.wait_ge(S["logit_ready"], n + 1)
                V.tensor_copy(logit[:, :, :].rearrange("p t e -> p (t e)"), bp[:, 0:NT * E]).then_inc(S["logit_sb"], 1)
                dve.wait_ge(S["logit_sb"], 5 * n + 1)
                V.tensor_reduce(lmax[:, :], logit[:, :, :], AX.X, ALU.max).then_inc(S["router_dve"], 1)
                mine = logit[:, :, :].unsqueeze(3).to_broadcast([P, NT, E, E])
                other = logit[:, :, :].unsqueeze(2).to_broadcast([P, NT, E, E])
                V.tensor_tensor(cmp_gt[:, :, :, :], other, mine, ALU.is_gt)
                V.tensor_tensor(cmp_eq[:, :, :, :], other, mine, ALU.is_equal).then_inc(S["logit_sb"], 1)
                dve.wait_ge(S["router_dve"], own + 1)
                V.tensor_tensor(ldiff[:, :, :], logit[:, :, :], lmax[:, :].unsqueeze(2).to_broadcast([P, NT, E]),
                                ALU.subtract).then_inc(S["router_dve"], 1)
                dve.wait_ge(S["const_ready"], 10)
                dve.wait_ge(S["logit_sb"], 5 * n + 2)
                V.tensor_tensor(cmp_eq[:, :, :, :].rearrange("p t a b -> p t (a b)"),
                                cmp_eq[:, :, :, :].rearrange("p t a b -> p t (a b)"),
                                before[:, :, :].rearrange("p a b -> p (a b)").unsqueeze(1)
                                .to_broadcast([P, NT, E * E]), ALU.mult).then_inc(S["logit_sb"], 1)
                dve.wait_ge(S["logit_sb"], 5 * n + 3)
                V.tensor_tensor(cmp_gt[:, :, :, :].rearrange("p t a b -> p (t a b)"),
                                cmp_gt[:, :, :, :].rearrange("p t a b -> p (t a b)"),
                                cmp_eq[:, :, :, :].rearrange("p t a b -> p (t a b)"), ALU.add).then_inc(S["logit_sb"], 1)
                dve.wait_ge(S["logit_sb"], 5 * n + 4)
                V.tensor_reduce(rank[:, :, :].rearrange("p t e -> p (t e)"),
                                cmp_gt[:, :, :, :].rearrange("p t a b -> p (t a) b"), AX.X, ALU.add)\
                    .then_inc(S["logit_sb"], 1)

            def route_weights(n):
                own = 3 * n
                dve.wait_ge(S["logit_sb"], 5 * n + 5)
                dve.wait_ge(S["lexp_ready"], n + 1)
                V.scalar_tensor_tensor(lsel[:, :, :].rearrange("p t e -> p (t e)"),
                                       rank[:, :, :].rearrange("p t e -> p (t e)"), 2.0,
                                       lexp[:, :, :].rearrange("p t e -> p (t e)"), ALU.is_lt, ALU.mult)\
                    .then_inc(S["router_dve"], 1)
                dve.wait_ge(S["router_dve"], own + 3)
                V.tensor_reduce(lsum[:, :], (lexp if n < 2 else lsel)[:, :, :], AX.X, ALU.add).then_inc(S["route_ready"], 1)
                dve.wait_ge(S["route_ready"], 3 * n + 1)
                V.reciprocal(lrec[:, :], lsum[:, :]).then_inc(S["route_ready"], 1)
                dve.wait_ge(S["route_ready"], 3 * n + 2)
                V.tensor_tensor(route[n % 2][:, :, :], lsel[:, :, :], lrec[:, :].unsqueeze(2).to_broadcast([P, NT, E]),
                                ALU.mult).then_inc(S["route_ready"], 1)

            def attention(n, k):
                g = n % 2
                if k == 0:
                    if n < 2:
                        dve.wait_ge(S[f"ld_x{g}"], 16)
                    else:
                        dve.wait_ge(S["x_ffn"], n - 1)
                    statistics(n, 0)
                if k == 1:
                    normalise(n, 0)
                if n < 2:
                    if 5 <= k < 5 + NT:
                        t = k - 5
                        i = NT * n + t
                        s = score_b[n][t % 2][:, :].rearrange("p (h k) -> p h k", k=KEYS)
                        dve.wait_ge(S["score_ready"], i + 1)
                        V.tensor_reduce(nmax[:, t, :], s, AX.X, ALU.max, negate=True).then_inc(S["nmax_ready"], 1)
                        dve.wait_ge(S["nmax_ready"], i + 1)
                        V.tensor_tensor(prob[n][:, t, :].rearrange("p (h k) -> p h k", k=KEYS), s,
                                        nmax[:, t, :].unsqueeze(2).to_broadcast([P, HEADS, KEYS]), ALU.add)\
                            .then_inc(S["shifted"], 1)
                    if K_SUM <= k < K_SUM + NT:
                        t = k - K_SUM
                        i = NT * n + t
                        dve.wait_ge(S["exp_ready"], i + 1)
                        V.tensor_reduce(psum_[:, t, :], prob[n][:, t, :].rearrange("p (h k) -> p h k", k=KEYS),
                                        AX.X, ALU.add).then_inc(S["sum_ready"], 1)
                        dve.wait_ge(S["sum_ready"], i + 1)
                        V.reciprocal(prec[:, t, :], psum_[:, t, :]).then_inc(S["rec_ready"], 1)
                    if k == K_RES:
                        residual_attention(n)
                        statistics(n, 1)
                    if k == K_RES + 1:
                        normalise(n, 1)
                    if k == K_RES + 2:
                        low_of_xT(n)
                    if k == K_ROUTER:
                        route_tokens(n)
                    if k == K_ROUTER + 1:
                        route_weights(n)
                else:
                    pr = prob1[:, :, 0:KEYS]
                    if k == 3:
                        s = bs[:, 0:NT * KEYS].rearrange("p (t k) -> p t k", k=KEYS)
                        dve.wait_ge(S["s1_ready"], n - 1)
                        if n == 3:
                            dve.wait_ge(S["s1_T"], 1)
                        V.tensor_tensor(pr, s, c1[:, g * KEYS:(g + 1) * KEYS].unsqueeze(1).to_broadcast([P, NT, KEYS]),
                                        ALU.add).then_inc(S["s1_bias"], 1)
                        dve.wait_ge(S["s1_bias"], n - 1)
                        V.tensor_reduce(nmax1[:, :], pr, AX.X, ALU.max, negate=True).then_inc(S["s1_nmax"], 1)
                        dve.wait_ge(S["s1_nmax"], n - 1)
                        V.tensor_tensor(pr, pr, nmax1[:, :].unsqueeze(2).to_broadcast([P, NT, KEYS]), ALU.add)\
                            .then_inc(S["s1_shift"], 1)
                    if k == 4:
                        dve.wait_ge(S["s1_exp"], n - 1)
                        V.tensor_reduce(sum1[:, :], pr, AX.X, ALU.add).then_inc(S["s1_sum"], 1)
                        dve.wait_ge(S["s1_sum"], n - 1)
                        V.reciprocal(rec1[:, :], sum1[:, :]).then_inc(S["s1_rec"], 1)
                        dve.wait_ge(S["s1_rec"], n - 1)
                        V.tensor_tensor(pr, pr, rec1[:, :].unsqueeze(2).to_broadcast([P, NT, KEYS]), ALU.mult)\
                            .then_inc(S["s1_prob"], 1)
                    if k == 6:
                        residual_attention(n)
                        statistics(n, 1)
                    if k == 7:
                        normalise(n, 1)
                    if k == 8:
                        low_of_xT(n)
                    if k == 9:
                        route_tokens(n)
                    if k == 10:
                        route_weights(n)

            def gate(n, k):
                layer, ff, e, t = n // 2, FF[n // 2], k // NT, k % NT
                y = MM1_STEPS * n + k
                kept, slot = HID_EXPERTS[layer], hid_slot(n, e)
                if t == 0 and n:
                    if layer and e + E * (n - 2) >= kept:
                        dve.wait_ge(S["hidT_ready"], chunks_before(2) + 2 * (e + E * (n - 2) - kept + 1))
                    else:
                        dve.wait_ge(S["hidT_ready"], chunks_before(n - 1) + min(NCH[0], ((slot + 1) * ff - 1) // P + 1))
                dve.wait_ge(S["act_ready"], y + 1)
                V.scalar_tensor_tensor(hid[:, t, slot * ff:(slot + 1) * ff], act_sb[:, y % NA, 0:ff],
                                       route[n % 2][:, t, e:e + 1], yb[y % NY][:, ff:2 * ff],
                                       ALU.mult, ALU.mult).then_inc(S["hid_ready"], 1)

            def experts(n, k):
                layer, g = n // 2, n % 2
                if k == 0:
                    dve.wait_ge(S["route_ready"], 3 * (n + 1))
                if k < MM1_STEPS:
                    gate(n, k)
                if k in TSTEP[n]:
                    c = chunks_before(n) + TSTEP[n].index(k)
                    dve.wait_ge(S["hidh_ready"], c + 1)
                    low(hid_t[1][:, c % 2, :], tbank(n, c - chunks_before(n))[:, :], hid_t[0][:, c % 2, :], "hidl_ready")
                if k == TAIL[n] + 2:
                    dve.wait_ge(S["oT_ready"], n + 1)
                    xv = x_sb[:, g * NT:(g + 1) * NT, :].rearrange("p t d -> p (t d)")
                    V.scalar_tensor_tensor(xv, bp[:, :], tg[:, 2 + layer:3 + layer], xv, ALU.mult, ALU.add)\
                        .then_inc(S["x_ffn"], 1)

            for expert_steps, attentions, _, _ in SLOTS:
                for n, k in expert_steps:
                    experts(n, k)
                for n, k in attentions:
                    attention(n, k)
                    if (n, k) == (0, 0):
                        feature_weights()
                    if (n, k) == (0, KEY_BLOCKS_STEP):
                        key_blocks()

        @block.tensor
        def _(pe):
            T = nc.tensor

            def product3(out, a, b, start=True, stop=True):
                T.matmul(out, a[0], b[0], start=start, stop=False)
                T.matmul(out, a[0], b[1], start=False, stop=False)
                return T.matmul(out, a[1], b[0], start=False, stop=stop)

            pe.wait_ge(S["const_ready"], 1)
            pe.wait_ge(S["ld_ctx"], 16)
            T.transpose(tb[:, 0:NG * KEYS], ctx_sb[:, :], ident[0:NG * KEYS, 0:NG * KEYS]).then_inc(S["ctxT_done"], 1)
            pe.wait_ge(S["const_ready"], 4)
            pe.wait_ge(S["ld_fm"], 32)
            T.matmul(bs[:, 128:384], rep[:, :], fm_t[:, :].unsqueeze(1).to_broadcast([HD, 32, HD]),
                     start=True, stop=True).then_inc(S["wzp_done"], 1)
            pe.wait_ge(S["wz_done"], 1)
            T.matmul(bs[:, 0:1], rep_sgn[:, :], fm_b[:, :], start=True, stop=True).then_inc(S["bz_done"], 1)
            pe.wait_ge(S["ctxT_sb"], 1)
            for g in range(2):
                last = T.matmul(bp[:, g * NG * KEYS:(g + 1) * NG * KEYS], wz[:, g, :], ctx_t[:, :], start=True, stop=True)
            last.then_inc(S["zk_done"], 1)

            def keep_clock(count):
                for _ in range(count):
                    T.matmul(yb[1][:, 0:P], ident[:, :], ident[:, :], start=True, stop=True)

            keep_clock(CLOCK_PRODUCTS[0])

            def fc_transposes():
                pe.wait_ge(S["fcp_done"], 2)
                for g in range(2):
                    last = T.transpose(tb[:, g * D:(g + 1) * D], fc_p[:, g].rearrange("n s h e -> n (s h e)"), ident[:, :])
                last.then_inc(S["fcT_done"], 1)

            def values_through_fc():
                pe.wait_ge(S["fcT_sb"], 1)
                pe.wait_ge(S["kbd_done"], 4)
                for b in range(NG):
                    for c in range(4):
                        rows = kbd[:, b, c // 2].rearrange("p h k -> p (h k)")[:, (c % 2) * P:(c % 2) * P + P]
                        last = T.matmul((ob, tb)[b][:, c * D:(c + 1) * D], rows, fc_t[:, c // 2, :], start=True, stop=True)
                    last.then_inc(S["v0_done"], 1)

            def layer1_products(i):
                if i == 0:
                    pe.wait_ge(S["ld_at"], 16 * 6)
                    pe.wait_ge(S["logit_sb"], 5 + 1)
                    T.transpose(bp[:, 0:D], wo[:, :], ident[:, :])
                    T.matmul(bp[:, D:2 * D], wk[:, :], wq[:, :], start=True, stop=True)
                    T.matmul(bp[:, 2 * D:2 * D + 1], wk[:, :], bq[:, :], start=True, stop=True).then_inc(S["l1_pe"], 1)
                elif i == 1:
                    pe.wait_ge(S["l1_sb"], 1)
                    pe.wait_ge(S["xl_ready"], 2)
                    T.matmul(bs[:, 0:D], wv[:, :], wo_t[:, :], start=True, stop=True)
                    T.matmul(bs[0:1, D:2 * D], bv[:, :], wo_t[:, :], start=True, stop=True)
                    T.matmul(bs[:, 256:256 + NG * KEYS], kq[:, :], ctx_t[:, :], start=True, stop=True)
                    T.matmul(bs[:, 384:384 + NG * KEYS], bqk[:, :].to_broadcast([D, P]), ctx_t[:, :], start=True, stop=True)\
                        .then_inc(S["l1_pe"], 1)
                else:
                    pe.wait_ge(S["l1_sb"], 2)
                    for b in range(NG):
                        o = bp[0:KEYS, b * D:(b + 1) * D]
                        T.matmul(o, ctx_t[:, b * KEYS:(b + 1) * KEYS], vo[:, :], start=True, stop=False)
                        last = T.matmul(o, ones[:, 0:KEYS], bvo[:, :], start=False, stop=True)
                    last.then_inc(S["l1_pe"], 1)

            def transpose_x(n, which):
                m = order_of_norm(n, which)
                pe.wait_ge(S["xn_ready"], NT * (m + 1))
                if which:
                    pe.wait_ge(S["x_att"], n + 1)
                    if n < 2:
                        pe.wait_ge(S["shifted"], NT)
                if n and (n, which) != (1, 0):
                    pe.wait_ge(S["xl_ready"], n)
                if m == 0:
                    pe.wait_ge(S["bz_done"], 2)
                if (n, which) == (2, 0):
                    pe.wait_ge(S["l1_sb"], 3)
                for t in range(NT):
                    last = T.transpose((bs if which else main_b[n])[:, t * P:(t + 1) * P], xn[:, t, :], ident[:, :])
                last.then_inc(S["xT_ready"], 1)

            def router(n):
                pe.wait_ge(S["xt_sb"], order_of_norm(n, 1) + 1)
                if n < 2:
                    pe.wait_ge(S["probT_sb"], NT)
                    if n:
                        pe.wait_ge(S["logit_sb"], 1)
                else:
                    pe.wait_ge(S["x_ffn"], n - 1)
                pe.wait_ge(S["ld_r"], 32)
                for t in range(NT):
                    last = T.matmul(bp[:, t * E:(t + 1) * E], xt[n % 2][:, t * P:(t + 1) * P], rw[:, n // 2, :],
                                    start=True, stop=True)
                last.then_inc(S["logit_ready"], 1)

            def attention(n, k):
                g = n % 2
                if k == 2:
                    transpose_x(n, 0)
                    if n == 0:
                        keep_clock(CLOCK_PRODUCTS[1])
                if n < 2:
                    if k == 3:
                        pe.wait_ge(S["xt_sb"], order_of_norm(n, 0) + 1)
                        pe.wait_ge(S["fk_done"], 1)
                        for h in range(2):
                            T.matmul((main_b[n], prob_b[n])[h][:, :], wz[:, h, :], xt[n][:, :], start=True, stop=True)\
                                .then_inc(S["z_ready"], 1)
                        if n == 0:
                            keep_clock(CLOCK_PRODUCTS[2])
                    if 5 <= k < 5 + NT:
                        t = k - 5
                        i = NT * n + t
                        if t == 0:
                            pe.wait_ge(S["kbd_done"], 4)
                            pe.wait_ge(S["qf_ready"], 2 * n + 2)
                        if t >= 2:
                            pe.wait_ge(S["shifted"], i - 1)
                        for h in range(2):
                            last = T.matmul(score_b[n][t % 2][:, h * 256:(h + 1) * 256], qf[n][:, h, t * P:(t + 1) * P],
                                            kbd[:, g, h].rearrange("p h k -> p (h k)"), start=True, stop=True)
                        last.then_inc(S["score_ready"], 1)
                    if K_PV <= k < K_PV + NT:
                        t = k - K_PV
                        pe.wait_ge(S["probT_sb"], NT * n + t + 1)
                        pe.wait_ge(S["v0_sb"], 2)
                        o = att_b[n][:, t * D:(t + 1) * D]
                        for c in range(4):
                            last = T.matmul(o, prob_t[:, t % 2, c, :], v0[:, g, c, :], start=(c == 0), stop=(c == 3))
                        if t == NT - 1:
                            last.then_inc(S["att_ready"], 1)
                    if K_T <= k < K_T + NT:
                        t = k - K_T
                        pe.wait_ge(S["prob_ready"], NT * n + t + 1)
                        if t:
                            pe.wait_ge(S["probT_sb"], NT * n + t)
                        for c in range(4):
                            last = T.transpose(prob_b[n][:, c * P:(c + 1) * P], prob[n][:, t, c * P:(c + 1) * P], ident[:, :])
                        last.then_inc(S["probT_ready"], 1)
                    if k == K_RES + 2:
                        transpose_x(n, 1)
                    if k == K_ROUTER:
                        router(n)
                else:
                    if k == 3:
                        pe.wait_ge(S["xt_sb"], order_of_norm(n, 0) + 1)
                        pe.wait_ge(S["l1_sb"], 3)
                        for t in range(NT):
                            o = bs[:, t * KEYS:(t + 1) * KEYS]
                            last = T.matmul(o, xt[g][:, t * P:(t + 1) * P], m1[:, g * KEYS:(g + 1) * KEYS],
                                            start=True, stop=True)
                        last.then_inc(S["s1_ready"], 1)
                    if k == 5:
                        pe.wait_ge(S["s1_prob"], n - 1)
                        pe.wait_ge(S["one_col"], 1)
                        for t in range(NT):
                            last = T.transpose(bp[0:KEYS + 1, t * P:(t + 1) * P], prob1[:, t, :], ident[:, :])
                        last.then_inc(S["s1_T"], 1)
                    if k == 6:
                        pe.wait_ge(S["s1_T_sb"], n - 1)
                        pe.wait_ge(S["ld_bo"], 32)
                        for t in range(NT):
                            last = T.matmul(bs[:, t * D:(t + 1) * D], prob1_t[:, t, :], v1[:, g, :], start=True, stop=True)
                        last.then_inc(S["att_ready"], 1)
                    if k == 8:
                        transpose_x(n, 1)
                    if k == 9:
                        router(n)

            def first_product(n, k):
                layer, t = n // 2, k % NT
                y = MM1_STEPS * n + k
                if y >= NY:
                    pe.wait_ge(S["hid_ready"], y - NY + 1)
                elif y == 0:
                    pe.wait_ge(S["x_att"], 2)
                product3(yb[y % NY][:, 0:2 * FF[layer]], [a[:, t * P:(t + 1) * P] for a in xf[n % 2]],
                         [v[:, k // NT, :, :].rearrange("p s f -> p (s f)") for v in (wa_h[layer], wa_l[layer])])\
                    .then_inc(S["y_ready"], 1)

            def experts(n, k):
                layer, ff = n // 2, FF[n // 2]
                if k < MM1_STEPS:
                    if k == 0:
                        pe.wait_ge(S["xh_ready"], n + 1)
                        pe.wait_ge(S["xl_ready"], n + 1)
                    pe.wait_ge(S["wsplit_h"], wa_pieces(layer, k // NT))
                    pe.wait_ge(S["wsplit_l"], wa_pieces(layer, k // NT))
                    first_product(n, k)
                if k in TSTEP[n]:
                    i = TSTEP[n].index(k)
                    c = chunks_before(n) + i
                    last_expert = (i * P + P - 1) // ff
                    pe.wait_ge(S["hid_ready"], MM1_STEPS * n + NT * (last_expert + 1))
                    if n == 3 and i:
                        pe.wait_ge(S["hidl_ready"], c - 1)
                        pe.wait_ge(S["xl_ready"], 4)
                    elif c:
                        pe.wait_ge(S["hidl_ready"], c)
                    col = hid_slot(n, last_expert) * ff + i * P - last_expert * ff
                    for t in range(NT):
                        last = T.transpose(tbank(n, i)[:, t * P:(t + 1) * P], hid[:, t, col:col + P], ident[:, :])
                    last.then_inc(S["hidT_ready"], 1)
                if k - M_DELAY in TSTEP[n]:
                    i = TSTEP[n].index(k - M_DELAY)
                    c = chunks_before(n) + i
                    pe.wait_ge(S["hidh_ready"], c + 1)
                    pe.wait_ge(S["hidl_ready"], c + 1)
                    pe.wait_ge(S["wsplit_l"], wb_pieces(layer, i))
                    if i == 0 and n:
                        pe.wait_ge(S["o_sb"], n)
                    product3(ob[:, :], [w[:, i, :] for w in (wb_h[layer], wb_l[layer])],
                             [h[:, c % 2, :] for h in hid_t], start=(i == 0), stop=(i == NCH[layer] - 1))\
                        .then_inc(S["mm2_done"], 1)
                if k == TAIL[n] + 2:
                    pe.wait_ge(S["o_sb"], n + 1)
                    if n < 3:
                        pe.wait_ge(S["logit_sb"], 5 * (n + 1) + 1)
                    for t in range(NT):
                        last = T.transpose(bp[:, t * P:(t + 1) * P], o_t[:, t * P:(t + 1) * P], ident[:, :])
                    last.then_inc(S["oT_ready"], 1)

            for expert_steps, attentions, _, parts in SLOTS:
                for n, k in expert_steps:
                    experts(n, k)
                for n, k in attentions:
                    attention(n, k)
                    if (n, k) == (0, VALUES_STEP):
                        fc_transposes()
                        values_through_fc()
                for i in parts:
                    layer1_products(i)


_INS = ['x', 'ctx_1024', 'g_xattn', 'g_ffn', 'L0_xattn_fm_w', 'L0_xattn_fm_b', 'L0_xattn_fc_w', 'L0_xattn_fc_b',
        'L0_ffn_router_weight', 'L0_ffn_w1', 'L0_ffn_w2', 'L1_xattn_Wk', 'L1_xattn_Wv', 'L1_xattn_bv',
        'L1_xattn_Wq', 'L1_xattn_bq', 'L1_xattn_Wo', 'L1_xattn_bo', 'L1_ffn_w_gate', 'L1_ffn_w1', 'L1_ffn_w3',
        'L1_ffn_w2']


def kernel(**inputs):
    import numpy as _np
    import concourse.bacc as _bacc
    from concourse import mybir as _mybir
    from concourse.bass_utils import run_bass_kernel_spmd as _run

    nc = _bacc.Bacc("TRN2", target_bir_lowering=False, num_devices=1)
    arrays, args = {}, []
    for name in _INS:
        a = _np.ascontiguousarray(inputs[name])
        arrays[f"in_{name}_dram"] = a
        args.append(nc.dram_tensor(f"in_{name}_dram", a.shape, _mybir.dt.from_np(a.dtype), kind="ExternalInput").ap())
    args.append(nc.dram_tensor("out_0_dram", (2, 512, 128), _mybir.dt.float32, kind="ExternalOutput").ap())
    build(nc, *args)
    r = _run(nc, [arrays], core_ids=[0])
    return r.results[0]["out_0_dram"]
```
